# Optimizing a Trainium2 kernel written in Bass

```python
import numpy as np
import jax
import jax.numpy as jnp

def _softmax(x, axis=-1):
    return jax.nn.softmax(x, axis=axis)
def _gelu(x):
    return jax.nn.gelu(x, approximate=True)
def _silu(x):
    return jax.nn.silu(x)
def _sigmoid(x):
    return jax.nn.sigmoid(x)
def _layernorm(x, axis=-1, eps=1e-5):
    m = jnp.mean(x, axis=axis, keepdims=True)
    v = jnp.var(x, axis=axis, keepdims=True)
    return (x - m) / jnp.sqrt(v + eps)
def _scatter_add(tgt, idx, src, axis=0):
    return tgt.at[idx].add(src)
def _segment_sum(src, seg, n):
    return jax.ops.segment_sum(src, seg, n)

kernel_name = 'mk_adj_resnorm_d1_adj_1024_4cbaf3'

def setup_inputs(seed: int = 0):
    np.random.seed(seed)
    _w = jnp.asarray
    def _rec_inputs():
        import jax
        import jax.numpy as jnp
        _gk = jax.random.key(seed)
        x = -0.0002928 + 1 * jax.random.normal(jax.random.fold_in(_gk, 1), (4096, 1024), jnp.float32)
        _w = (1.0 + jnp.arange(4096, dtype=jnp.float32)) ** -0.5
        _w = _w / _w.mean()
        _pij = jnp.clip(0.0078125 * _w[:, None] * _w[None, :], 0.0, 1.0)
        _a = jax.random.uniform(jax.random.fold_in(_gk, 2), (4096, 4096)) < _pij
        _af = _a.astype(jnp.float32)
        adj = _af
        return x, adj
    x, adj = _rec_inputs()
    def _L0_gnn_setup():
        import jax, jax.numpy as jnp
        import numpy as np
        N = 4096
        D_IN = 1024
        H = 16
        DH = D_IN // H
        ALPHA = 0.2
        MASK_VAL = -65500.0
        key = jax.random.key(seed)
        ks = jax.random.split(key, 7)
        x = jax.random.normal(ks[0], (N, D_IN), dtype=jnp.float32)
        adj = jax.random.randint(ks[1], (N, N), 0, 2).astype(jnp.float32)
        s = 1.0 / np.sqrt(D_IN)
        W_seq = jax.random.normal(ks[2], (D_IN, D_IN), dtype=jnp.float32) * s
        a1 = jax.random.normal(ks[3], (DH,), dtype=jnp.float32) / np.sqrt(DH)
        a2 = jax.random.normal(ks[4], (DH,), dtype=jnp.float32) / np.sqrt(DH)
        W_out = jax.random.normal(ks[5], (D_IN, D_IN), dtype=jnp.float32) * s
        b_out = jax.random.normal(ks[6], (D_IN,), dtype=jnp.float32) * 0.01
        return {'x': x, 'adj': adj, 'W_seq': W_seq, 'a1': a1, 'a2': a2, 'W_out': W_out, 'b_out': b_out}
    _L0_gnn_all = _L0_gnn_setup()
    _L0_gnn_in = {k: v for k, v in _L0_gnn_all.items() if k in ('W_seq', 'a1', 'a2', 'W_out', 'b_out', )}
    del _L0_gnn_all

    return {
        "x": x,
        "adj": adj,
        "L0_gnn_W_seq": _L0_gnn_in["W_seq"],
        "L0_gnn_a1": _L0_gnn_in["a1"],
        "L0_gnn_a2": _L0_gnn_in["a2"],
        "L0_gnn_W_out": _L0_gnn_in["W_out"],
        "L0_gnn_b_out": _L0_gnn_in["b_out"],
    }

def reference(x, adj, L0_gnn_W_seq, L0_gnn_a1, L0_gnn_a2, L0_gnn_W_out, L0_gnn_b_out):
    import jax
    import jax.numpy as jnp
    def _L0_gnn_ref(x, adj, W_seq, a1, a2, W_out, b_out):
        import jax, jax.numpy as jnp
        import numpy as np
        N = 4096
        D_IN = 1024
        H = 16
        DH = D_IN // H
        ALPHA = 0.2
        MASK_VAL = -65500.0
        seq = (x @ W_seq).reshape(N, H, DH)
        score1 = jnp.einsum('nhd,d->hn', seq, a1)
        score2 = jnp.einsum('nhd,d->hn', seq, a2)
        scores = score1[:, :, None] + score2[:, None, :]
        scores = jax.nn.leaky_relu(scores, negative_slope=ALPHA)
        scores = scores + (1.0 - adj)[None, :, :] * MASK_VAL
        attn = jax.nn.softmax(scores, axis=-1)
        hidden = jnp.einsum('hij,jhd->ihd', attn, seq).reshape(N, D_IN)
        hidden = hidden @ W_out + b_out
        return jax.nn.elu(hidden)

    x = _layernorm(x + _L0_gnn_ref(x, adj, L0_gnn_W_seq, L0_gnn_a1, L0_gnn_a2, L0_gnn_W_out, L0_gnn_b_out), axis=-1)
    return x


_drawn_inputs = setup_inputs


def setup_inputs(seed=0):
    import zlib

    import numpy as np

    out = dict(_drawn_inputs(seed))
    spreads = {}
    factors = {'L0_gnn_b_out': 6.155}
    for name, (base, spread) in spreads.items():
        noise = np.random.default_rng([zlib.crc32(name.encode()), seed]).standard_normal(out[name].shape)
        drawn = base * np.exp(spread * noise) if base else spread * noise
        out[name] = jnp.asarray(drawn.astype(out[name].dtype))
    for name, factor in factors.items():
        out[name] = (out[name] * factor).astype(out[name].dtype)
    return out
```

```python
import math
from contextlib import ExitStack

import concourse.bass as bass
from concourse import mybir

F32 = mybir.dt.float32
F16 = mybir.dt.float16
BF16 = mybir.dt.bfloat16
F8 = mybir.dt.float8e4
U8 = mybir.dt.uint8
I8 = mybir.dt.int8
U16 = mybir.dt.uint16
ALU = mybir.AluOpType
ACT = mybir.ActivationFunctionType
AX = mybir.AxisListType

P = 128
N, D, H = 4096, 1024, 16
DH = D // H
NT = N // P
KT = D // P
HALF = D // 2
HH = H // 2
BLK = 8
BN = BLK * P
NB = N // BN
G = H * NB
NQ = NT // 2
V1 = DH + 1
V2 = 2 * V1
CT = NT // NB
EPS = 1e-5
W_SCALE = 256.0
H_SCALE = 16.0
V_SCALE = 2.0 ** 15
MASK_ONE = 64.0
RS = 9
DMA = 16


def build(nc, x, adj, w_seq, a1, a2, w_out, b_out, out):
    seq_d = nc.dram_tensor("seq_d", (N, D), F32).ap()
    hid_d = nc.dram_tensor("hid_d", (N, D), F32).ap()
    s1_d = nc.dram_tensor("s1_d", (H * NT, P), F32).ap()

    x_t = x.rearrange("(t p) c -> t p c", p=P)
    adj_t = adj.rearrange("(t p) c -> t p c", p=P)
    out_t = out.rearrange("(t p) c -> t p c", p=P)
    seq_st = seq_d.rearrange("(t p) c -> t p c", p=P)
    hid_t = hid_d.rearrange("(t p) c -> t p c", p=P)
    seq_ld = seq_d.rearrange("(b t p) (h d) -> h b p t d", p=P, t=CT, d=DH)
    hid_st = hid_d.rearrange("(b t p) (h d) -> h b p t d", p=P, t=BLK, d=DH)
    s1_g = s1_d.rearrange("(g t) p -> g (t p)", t=BLK)

    ctx = ExitStack()
    with ctx:
        def sb(name, shape, dt, c=None):
            return (c or ctx).enter_context(nc.sbuf_tensor(name, shape, dt))

        def sem(name):
            return ctx.enter_context(nc.semaphore(name))

        ident_b = sb("ident_b", [P, P], BF16)
        ident_f = sb("ident_f", [P, P], F32)
        ph13 = ExitStack()
        adjT = sb("adjT", [P, NT, N], U8, ph13)
        s1 = sb("s1", [P, H, NT], F32, ph13)
        s2 = sb("s2", [P, H, NT], F32, ph13)
        stat = sb("stat", [P, 2, H], F32, ph13)
        stat_r = sb("stat_r", [P, 2, H], F32, ph13)
        ph1 = ExitStack()
        w_hi = sb("w_hi", [P, KT, D], F16, ph1)
        w_lo = sb("w_lo", [P, KT, D], F16, ph1)
        xin = sb("xin", [P, 2, D], F32, ph1)
        xT_hi = sb("xT_hi", [P, 2, D], F16, ph1)
        xT_lo = sb("xT_lo", [P, 2, D], F16, ph1)
        seq_o = sb("seq_o", [P, D], F32, ph1)
        prod = sb("prod", [P, HALF], F32, ph1)
        adj_in = sb("adj_in", [P, 2, N], BF16, ph1)
        a_row = sb("a_row", [P, 2, DH], F32, ph1)
        smax = sb("smax", [P, H, NT], F32, ph1)
        degree = sb("degree", [P, 2], F32, ph1)
        lonely = sb("lonely", [P, 1], F32, ph1)
        ph1.close()
        ph3 = ExitStack()
        ns2, rowA = s2, s1
        rowC = sb("rowC", [P, H, NT], F32, ph3)
        colB = sb("colB", [P, 2, H, NT], F32, ph3)
        rhs = sb("rhs", [P, 2, NT, 2, V2], F16, ph3)
        s1row = sb("s1row", [P, 2, BN], F32, ph3)
        cmp = sb("cmp", [P, 2, 2, BN], U8, ph3)
        pos = sb("pos", [P, 2, 2, BN], U8, ph3)
        neg = sb("neg", [P, 2, 2, BN], U8, ph3)
        stage = sb("stage", [P, 2, CT, DH], F32, ph3)
        vbuf = sb("vbuf", [P, CT, V1], F32, ph3)
        mix = sb("mix", [P, BLK, V2], F32, ph3)
        vcol = sb("vcol", [P, 2, CT], F32, ph3)
        hout = sb("hout", [P, BLK, DH], F32, ph3)
        den = sb("den", [P, 3, BLK], F32, ph3)
        amax = sb("amax", [P, H], F32, ph3)
        ginv = sb("ginv", [P, H], F32, ph3)
        ph3.close()
        tmpa = rhs[:, 0, 0:4 * H * NT // V2 // 2 + 2, :, :].rearrange("p a b c -> p (a b c)")[
            :, 0:4 * H * NT].bitcast(F32).rearrange("p (r h t) -> p r h t", r=2, t=NT)
        s1T = cmp[:, :, :, :].rearrange("p a b c -> p (a b c)")[:, 0:4 * 4 * P].bitcast(F32)\
            .rearrange("p (k c) -> p k c", k=4)
        ph13.close()
        ph4 = ExitStack()
        o_hi = sb("o_hi", [P, KT, D], F16, ph4)
        o_lo = sb("o_lo", [P, KT, D], F16, ph4)
        o_in = sb("o_in", [P, KT, D], F32, ph4)
        hin = sb("hin", [P, 2, D], F32, ph4)
        xres = sb("xres", [P, 2, D], F32, ph4)
        hT_hi = sb("hT_hi", [P, 2, D], F16, ph4)
        hT_lo = sb("hT_lo", [P, 2, D], F16, ph4)
        b_row = sb("b_row", [P, D], F32, ph4)
        zbuf = sb("zbuf", [P, 2, D], F32, ph4)
        ebuf = sb("ebuf", [P, 2, D], F32, ph4)
        ybuf = sb("ybuf", [P, 2, D], F32, ph4)
        bnst = sb("bnst", [P, 2, 6], F32, ph4)
        mv = sb("mv", [P, 2], F32, ph4)
        nmr = sb("nmr", [P, 2, 2], F32, ph4)
        rstd = sb("rstd", [P, 2], F32, ph4)
        minus_half = sb("minus_half", [P, 1], F32, ph4)
        ph4.close()

        ps = ctx.enter_context(nc.psum_tensor("ps", [P, 8, HALF], F32))
        xT_ps = ps[:, 0:2, :].rearrange("p a c -> p (a c)")
        adjT_ps = [ps[:, 2 + b, :].bitcast(BF16).rearrange("p (g c) -> p g c", c=P) for b in range(2)]
        proj_ps = [ps[:, 4 + b, :] for b in range(4)]

        names = """ident_made a_loaded w_hi_made w_split
            degree_made lonely_made adj_fixed xT_written xhi_made xlo_made adjT_written adjT_act
            adjT_dve proj_written seq_copied seq_reduced prod_made score_made
            stat_made stat_reduced ginv_made expin_made exp_made s1T_written s1T_copied
            s1_stored cmp_act cmp_dve pos_made neg_made pos_used neg_used rhs_step
            bank_ready bank_free mixA_made parts_added den_made den_step hout_made hid_stored wo_loaded wo_hi_made wo_split b_loaded
            half_made hT_written hhi_made hlo_made o_written
            z_made e_in_made e_made y_made y2_made bn_made mv_made rstd_made nmr_made yn_made
            """.split()
        s = type("Sems", (), {n: sem(n) for n in names})
        w_loaded, x_loaded, adj_loaded, seq_stored, stage_loaded, s1row_loaded, hin_loaded, \
            xres_loaded, o_stored = ([sem(f"{n}_{u}") for u in range(2)] for n in (
                "w_loaded", "x_loaded", "adj_loaded", "seq_stored", "stage_loaded", "s1row_loaded",
                "hin_loaded", "xres_loaded", "o_stored"))

        tally = {e: sem(e + "_tally") for e in ("sp", "act", "dve", "pe")}

        def wait_alone(eng, name, semaphore, value):
            eng.wait_ge(semaphore, value)
            eng.sem_inc(tally[name], 1)

        def row_loads(g, slot):
            return (g - slot) * (DMA // 2) + DMA

        block = ctx.enter_context(nc.Block())

        @block.sync
        def _(sp):
            sp.dma_start(a_row[:, 0, :], a1.partition_broadcast(P)).then_inc(s.a_loaded, DMA)
            sp.dma_start(a_row[:, 1, :], a2.partition_broadcast(P)).then_inc(s.a_loaded, DMA)
            for k in range(KT):
                if k >= 2:
                    sp.wait_ge(s.w_split, k - 1)
                sp.dma_start(xin[:, k % 2, :], w_seq[k * P:(k + 1) * P, :]).then_inc(w_loaded[k % 2], DMA)
            sp.wait_ge(s.w_split, KT - 1)
            sp.dma_start(xin[:, 0, :], x_t[0, :, :]).then_inc(x_loaded[0], DMA)
            sp.wait_ge(s.w_split, KT)
            sp.dma_start(xin[:, 1, :], x_t[1, :, :]).then_inc(x_loaded[1], DMA)
            with sp.Fori(1, NT // 2) as r:
                for u in range(2):
                    sp.wait_ge(s.xT_written, 2 * r + u - 1)
                    sp.dma_start(xin[:, u, :], x_t[2 * r + u, :, :]).then_inc(x_loaded[u], DMA)
            sp.wait_ge(s.s1T_copied, 1)
            sp.dma_start(s1_d.rearrange("(k r) c -> r k c", r=P), s1T).then_inc(s.s1_stored, DMA)
            for n in range(2):
                sp.wait_ge(seq_stored[n], (NT + 1) * DMA)

            def load_stage(head, part, slot):
                sp.dma_start(stage[:, slot, :, :], seq_ld[head, part, :, :, :]).then_inc(stage_loaded[slot], DMA)

            sp.wait_ge(s.s1T_written, 1)
            load_stage(0, 0, 0)
            load_stage(0, 1, 1)
            sp.wait_ge(s.s1_stored, DMA)

            def load_row(g, slot):
                sp.dma_start(s1row[:, slot, :], s1_g[g, :].partition_broadcast(P)).then_inc(s1row_loaded[slot], DMA)

            load_row(0, 0)
            load_row(1, 1)
            for c in range(2, 6):
                sp.wait_ge(s.rhs_step, RS * (c - 1))
                load_stage(c // NB, c % NB, c % 2)

            def store_hidden(head, part, g):
                sp.wait_ge(s.hout_made, g + 1)
                sp.dma_start(hid_st[head, part, :, :, :], hout[:, :, :]).then_inc(s.hid_stored, DMA)

            def next_row(g, slot):
                wait_alone(sp, "sp", s.cmp_act, (g + 1) * (NT * 3 // 4))
                wait_alone(sp, "sp", s.cmp_dve, (g + 1) * (NT // 4))
                load_row(g + 2, slot)

            with sp.Fori(0, H - 2) as hd:
                for b in range(NB):
                    g, c = hd * NB + b, b + 6
                    store_hidden(hd, b, g)
                    next_row(g, b % 2)
                    sp.wait_ge(s.rhs_step, RS * (g + 5))
                    load_stage(hd + c // NB, c % NB, c % 2)
            for g in range(G - 2 * NB, G):
                store_hidden(g // NB, g % NB, g)
                if g + 2 < G:
                    next_row(g, g % 2)
                if g + 6 < G:
                    sp.wait_ge(s.rhs_step, RS * (g + 5))
                    load_stage((g + 6) // NB, (g + 6) % NB, g % 2)
            sp.wait_ge(s.bank_ready, BLK * G)
            sp.wait_ge(s.hid_stored, G * DMA)
            sp.dma_start(o_in[:, :, :], w_out.rearrange("(k p) c -> p k c", p=P)).then_inc(s.wo_loaded, DMA)
            sp.dma_start(b_row[:, :], b_out.partition_broadcast(P)).then_inc(s.b_loaded, DMA)

            def load_out(t, u):
                sp.dma_start(hin[:, u, :], hid_t[t, :, :]).then_inc(hin_loaded[u], DMA)
                sp.dma_start(xres[:, u, :], x_t[t, :, :]).then_inc(xres_loaded[u], DMA)

            load_out(0, 0)
            load_out(1, 1)
            with sp.Fori(1, NT // 2) as r:
                for u in range(2):
                    sp.wait_ge(s.hT_written, 2 * r + u - 1)
                    sp.wait_ge(s.y_made, 2 * r + u - 1)
                    load_out(2 * r + u, u)
            for u in range(2):
                sp.wait_ge(o_stored[u], (NT // 2 + 1) * DMA)

        @block.gpsimd
        def _(pool):
            for i, m in enumerate((ident_b, ident_f)):
                nc.gpsimd.memset(m[:, :], 0.0).then_inc(s.ident_made, 1)
                pool.wait_ge(s.ident_made, 2 * i + 1)
                nc.gpsimd.affine_select(out=m[:, :], in_=m[:, :], compare_op=ALU.not_equal, fill=1.0,
                                        base=0, pattern=[[-1, P]], channel_multiplier=1)\
                    .then_inc(s.ident_made, 1)
            for u in range(2):
                pool.dma_start(adj_in[:, u, :], adj_t[u, :, :]).then_inc(adj_loaded[u], DMA)
            with pool.Fori(1, NT // 2) as r:
                for u in range(2):
                    pool.wait_ge(s.adjT_written, 4 * (2 * r + u - 1))
                    pool.dma_start(adj_in[:, u, :], adj_t[2 * r + u, :, :]).then_inc(adj_loaded[u], DMA)
            pool.wait_ge(s.stat_made, 2)
            nc.gpsimd.partition_all_reduce(stat_r[:, :, :], stat[:, :, :], P, bass.bass_isa.ReduceOp.max)\
                .then_inc(s.stat_reduced, 1)
            pool.wait_ge(s.exp_made, 3)
            pool.wait_ge(s.ginv_made, 2)

            def chunk(c, head, part, par, slot):
                pool.wait_ge(stage_loaded[slot], (c // 2 + 1) * DMA if isinstance(c, int) else
                             (head * (NB // 2) + part // 2 + 1) * DMA)
                if not isinstance(c, int):
                    pool.wait_ge(s.bank_ready, BLK * NB * (head - 1))
                ts = bass.ds(part * CT, CT)
                nc.gpsimd.tensor_tensor(vcol[:, :, :], colB[:, :, head, ts],
                                        ginv[:, bass.ds(head, 1)].unsqueeze(2).to_broadcast([P, 2, CT]),
                                        ALU.mult).then_inc(s.rhs_step, 1)
                pool.wait_ge(s.rhs_step, RS * c + 1)
                for br in range(2):
                    n = RS * c + 1 + 4 * br
                    nc.gpsimd.tensor_tensor(vbuf[:, :, 0:DH], stage[:, slot, :, :],
                                            vcol[:, br, :].unsqueeze(2).to_broadcast([P, CT, DH]),
                                            ALU.mult).then_inc(s.rhs_step, 1)
                    nc.gpsimd.tensor_copy(vbuf[:, :, DH], colB[:, br, head, ts]).then_inc(s.rhs_step, 1)
                    pool.wait_ge(s.rhs_step, n + 2)
                    nc.gpsimd.tensor_copy(rhs[:, par, ts, br, 0:V1], vbuf[:, :, :]).then_inc(s.rhs_step, 1)
                    pool.wait_ge(s.rhs_step, n + 3)
                    nc.gpsimd.tensor_tensor(rhs[:, par, ts, br, V1:V2], vbuf[:, :, :],
                                            rhs[:, par, ts, br, 0:V1], ALU.subtract)\
                        .then_inc(s.rhs_step, 1)
                    pool.wait_ge(s.rhs_step, n + 4)

            for c in range(NB):
                chunk(c, 0, c, 0, c % 2)

            def combine(g):
                pool.wait_ge(s.bank_free, BLK * (g + 2))
                both = mix[:, :, 0:DH]
                nc.gpsimd.tensor_tensor(both, both, mix[:, :, V1:V1 + DH], ALU.add)\
                    .then_inc(s.parts_added, 1)
                pool.wait_ge(s.parts_added, g + 1)
                pool.wait_ge(s.den_made, g + 1)
                if not isinstance(g, int) or g > 0:
                    pool.wait_ge(s.hid_stored, g * DMA)
                nc.gpsimd.tensor_tensor(hout[:, :, :], both,
                                        den[:, 2, :].unsqueeze(2).to_broadcast([P, BLK, DH]), ALU.mult)\
                    .then_inc(s.hout_made, 1)

            for b in range(NB):
                chunk(b + NB, 1, b, 1, b % 2)
                combine(b)
            with pool.Fori(1, H - 1) as hd:
                par = (hd + 1) % 2
                for b in range(NB):
                    chunk((hd + 1) * NB + b, hd + 1, b, par, b % 2)
                    combine(hd * NB + b)
            for b in range(NB):
                combine((H - 1) * NB + b)
            pool.wait_ge(s.hid_stored, G * DMA)
            nc.gpsimd.memset(minus_half[:, :], -0.5).then_inc(s.half_made, 1)
            pool.wait_ge(s.half_made, 1)
            with pool.Fori(0, NT // 2) as r:
                for u in range(2):
                    t = 2 * r + u
                    pool.wait_ge(s.mv_made, 2 * t + 2)
                    nc.gpsimd.tensor_tensor(rstd[:, u:u + 1], mv[:, 1:2], minus_half[:, :], ALU.pow)\
                        .then_inc(s.rstd_made, 1)

        @block.scalar
        def _(act):
            for k in range(KT):
                act.wait_ge(w_loaded[k % 2], (k // 2 + 1) * DMA)
                nc.scalar.activation(w_hi[:, k, :], xin[:, k % 2, :], ACT.Copy, scale=W_SCALE)\
                    .then_inc(s.w_hi_made, 1)
            with act.Fori(0, NT // 2) as r:
                for u in range(2):
                    t = 2 * r + u
                    act.wait_ge(adj_loaded[u], (r + 1) * DMA)
                    nc.scalar.activation(adj_in[:, u, :], adj_in[:, u, :], ACT.Copy,
                                         accum_out=degree[:, u:u + 1]).then_inc(s.degree_made, 1)
                    act.wait_ge(s.xT_written, t + 1)
                    nc.scalar.activation(xT_hi[:, u, :], xT_ps, ACT.Copy).then_inc(s.xhi_made, 1)
                    for g in (0, 2):
                        act.wait_ge(s.adjT_written, 4 * t + g + 1)
                        nc.scalar.activation(adjT[:, 8 * g:8 * g + 8, bass.ds(t * P, P)], adjT_ps[0],
                                             ACT.Copy).then_inc(s.adjT_act, 1)
                    for n in range(2):
                        act.wait_ge(s.proj_written, 2 * t + n + 1)
                        act.wait_ge(s.seq_reduced, 2 * t + n + 1)
                        act.wait_ge(seq_stored[n], (t + 1) * DMA)
                        nc.scalar.activation(seq_o[:, n * HALF:(n + 1) * HALF], proj_ps[2 * u + n],
                                             ACT.Copy, scale=1.0 / W_SCALE).then_inc(s.seq_copied, 1)
                        act.wait_ge(s.seq_copied, 2 * t + n + 1)
                        act.dma_start(seq_st[t, :, n * HALF:(n + 1) * HALF],
                                      seq_o[:, n * HALF:(n + 1) * HALF]).then_inc(seq_stored[n], DMA)
            act.wait_ge(s.s1T_written, 1)
            for n in range(2):
                act.wait_ge(seq_stored[n], (NT + 1) * DMA)
            nc.scalar.activation(s1T, ps[:, 0, :].rearrange("p (k c) -> p k c", k=4), ACT.Copy)\
                .then_inc(s.s1T_copied, 1)
            act.wait_ge(s.expin_made, 2)
            nc.scalar.activation(rowA[:, :, :], rowA[:, :, :], ACT.Exp).then_inc(s.exp_made, 1)
            nc.scalar.activation(rowC[:, :, :], rowC[:, :, :], ACT.Exp).then_inc(s.exp_made, 1)
            act.wait_ge(s.expin_made, 4)
            nc.scalar.activation(colB[:, :, :, :], colB[:, :, :, :], ACT.Exp).then_inc(s.exp_made, 1)
            act.wait_ge(s.s1_stored, DMA)

            def compare(slot_row, head, j, slot, jj):
                nc.scalar.activation(cmp[:, slot, jj, :].bitcast(I8), s1row[:, slot_row, :], ACT.Sign,
                                     scale=-1.0, bias=ns2[:, head, j:j + 1]).then_inc(s.cmp_act, 1)

            def pairs(g, head, slot_row, qs):
                for q in qs:
                    if q == 0:
                        act.wait_ge(s1row_loaded[slot_row], row_loads(g, slot_row))
                    if not (isinstance(g, int) and g == 0 and q < 2):
                        wait_alone(act, "act", s.pos_made, NQ * g + q - 1)
                    compare(slot_row, head, 2 * q, q % 2, 0)
                    if q % 2 == 0:
                        compare(slot_row, head, 2 * q + 1, q % 2, 1)

            def evacuate(g, head, part):
                if not isinstance(g, int) or g > 0:
                    act.wait_ge(s.hout_made, g)
                for k in range(BLK):
                    act.wait_ge(s.bank_ready, BLK * g + k + 1)
                    nc.scalar.activation(mix[:, k, :], ps[:, k, 0:V2], ACT.Copy,
                                         scale=rowA[:, head, bass.ds(part * BLK + k, 1)])\
                        .then_inc(s.mixA_made, 1)

            act.wait_ge(s.exp_made, 3)
            act.wait_ge(s.ginv_made, 1)
            pairs(0, 0, 0, (0, 1))
            pairs(0, 0, 0, range(2, NQ))
            pairs(1, 0, 1, (0, 1))
            evacuate(0, 0, 0)
            with act.Fori(0, H - 1) as hd:
                for b in range(1, NB + 1):
                    g = hd * NB + b
                    h_, b_ = hd + b // NB, b % NB
                    pairs(g, h_, b % 2, range(2, NQ))
                    pairs(g + 1, hd + (b + 1) // NB, (b + 1) % 2, (0, 1))
                    evacuate(g, h_, b_)
            for g in range(G - NB + 1, G):
                pairs(g, H - 1, g % 2, range(2, NQ))
                if g + 1 < G:
                    pairs(g + 1, H - 1, (g + 1) % 2, (0, 1))
                evacuate(g, H - 1, g % NB)
            act.wait_ge(s.wo_loaded, DMA)
            for k in range(KT):
                nc.scalar.activation(o_hi[:, k, :], o_in[:, k, :], ACT.Copy, scale=W_SCALE)\
                    .then_inc(s.wo_hi_made, 1)
            with act.Fori(0, NT // 2) as r:
                for u in range(2):
                    t = 2 * r + u
                    act.wait_ge(s.hT_written, t + 1)
                    nc.scalar.activation(hT_hi[:, u, :], xT_ps, ACT.Copy, scale=H_SCALE)\
                        .then_inc(s.hhi_made, 1)
                    act.wait_ge(s.e_in_made, t + 1)
                    nc.scalar.activation(ebuf[:, u, :], ebuf[:, u, :], ACT.Exp).then_inc(s.e_made, 1)
                    act.wait_ge(s.nmr_made, t + 1)
                    nc.scalar.activation(ybuf[:, u, :], ybuf[:, u, :], ACT.Identity,
                                         scale=rstd[:, u:u + 1], bias=nmr[:, u, 0:1]).then_inc(s.yn_made, 1)
                    act.wait_ge(s.yn_made, t + 1)
                    act.dma_start(out_t[t, :, :], ybuf[:, u, :]).then_inc(o_stored[u], DMA)

        @block.vector
        def _(dve):
            nc.vector.sem_inc(s.seq_reduced, 2)
            for n in range(2):
                nc.vector.sem_inc(seq_stored[n], DMA)
            for k in range(KT):
                dve.wait_ge(s.w_hi_made, k + 1)
                nc.vector.scalar_tensor_tensor(out=w_lo[:, k, :], in0=xin[:, k % 2, :], scalar=W_SCALE,
                                               in1=w_hi[:, k, :], op0=ALU.mult, op1=ALU.subtract)\
                    .then_inc(s.w_split, 1)
            dve.wait_ge(s.a_loaded, 2 * DMA)
            with dve.Fori(0, NT // 2) as r:
                for u in range(2):
                    t = 2 * r + u
                    dve.wait_ge(s.degree_made, t + 1)
                    nc.vector.tensor_scalar(lonely[:, :], degree[:, u:u + 1], 0.0, None, ALU.is_equal)\
                        .then_inc(s.lonely_made, 1)
                    dve.wait_ge(s.lonely_made, t + 1)
                    nc.vector.tensor_scalar(adj_in[:, u, :], adj_in[:, u, :], lonely[:, 0:1], MASK_ONE,
                                            ALU.max, ALU.mult).then_inc(s.adj_fixed, 1)
                    dve.wait_ge(s.xhi_made, t + 1)
                    nc.vector.tensor_tensor(xT_lo[:, u, :], xT_ps, xT_hi[:, u, :], ALU.subtract)\
                        .then_inc(s.xlo_made, 1)
                    for g in (1, 3):
                        dve.wait_ge(s.adjT_written, 4 * t + g + 1)
                        nc.vector.tensor_copy(adjT[:, 8 * g:8 * g + 8, bass.ds(t * P, P)], adjT_ps[1])\
                            .then_inc(s.adjT_dve, 1)
                    for n in range(2):
                        dve.wait_ge(s.seq_copied, 2 * t + n + 1)
                        half = seq_o[:, n * HALF:(n + 1) * HALF].rearrange("p (h d) -> p h d", d=DH)
                        pr = prod[:, :].rearrange("p (h d) -> p h d", d=DH)
                        hs = slice(n * HH, (n + 1) * HH)
                        for v, dst in ((0, s1), (1, s2)):
                            i = 4 * t + 2 * n + v
                            nc.vector.tensor_tensor(pr, half, a_row[:, v, :].unsqueeze(1)
                                                    .to_broadcast([P, HH, DH]), ALU.mult)\
                                .then_inc(s.prod_made, 1)
                            dve.wait_ge(s.prod_made, i + 1)
                            nc.vector.tensor_reduce(dst[:, hs, bass.ds(t, 1)].rearrange("p h o -> p (h o)"),
                                                    pr, AX.X, ALU.add).then_inc(s.score_made, 1)
                            dve.wait_ge(s.score_made, i + 1)
                        nc.vector.tensor_reduce(smax[:, hs, bass.ds(t, 1)].rearrange("p h o -> p (h o)"),
                                                half, AX.X, ALU.max, apply_absolute_value=True)\
                            .then_inc(s.seq_reduced, 1)
            dve.wait_ge(s.seq_reduced, 2 * NT + 2)
            dve.wait_ge(s.score_made, 4 * NT)
            nc.vector.tensor_reduce(stat[:, 0, :], s2[:, :, :], AX.X, ALU.max).then_inc(s.stat_made, 1)
            nc.vector.tensor_reduce(stat[:, 1, :], smax[:, :, :], AX.X, ALU.max).then_inc(s.stat_made, 1)
            dve.wait_ge(s.stat_reduced, 1)
            dve.wait_ge(s.s1T_written, 1)
            for n in range(2):
                dve.wait_ge(seq_stored[n], (NT + 1) * DMA)
            top = stat_r[:, 0, :].unsqueeze(2).to_broadcast([P, H, NT])
            nc.vector.tensor_scalar(amax[:, :], stat_r[:, 1, :], 1e-30, None, ALU.max).then_inc(s.den_step, 1)
            nc.vector.tensor_tensor(tmpa[:, 0, :, :], s1[:, :, :], top, ALU.add).then_inc(s.den_step, 1)
            nc.vector.tensor_tensor(tmpa[:, 1, :, :], s2[:, :, :], top, ALU.subtract).then_inc(s.den_step, 1)
            dve.wait_ge(s.den_step, 3)
            nc.vector.tensor_scalar(rowA[:, :, :], tmpa[:, 0, :, :], 0.8, 0.0, ALU.mult, ALU.min)\
                .then_inc(s.expin_made, 1)
            nc.vector.tensor_scalar(rowC[:, :, :], tmpa[:, 0, :, :], -0.8, 0.0, ALU.mult, ALU.min)\
                .then_inc(s.expin_made, 1)
            nc.vector.tensor_scalar(colB[:, 0, :, :], tmpa[:, 1, :, :], math.log(V_SCALE), None, ALU.add)\
                .then_inc(s.expin_made, 1)
            nc.vector.tensor_scalar(colB[:, 1, :, :], tmpa[:, 1, :, :], 0.2, math.log(V_SCALE),
                                    ALU.mult, ALU.add).then_inc(s.expin_made, 1)
            nc.vector.tensor_scalar(ns2[:, :, :], s2[:, :, :], -1.0, None, ALU.mult).then_inc(s.ginv_made, 1)
            nc.vector.reciprocal(ginv[:, :], amax[:, :]).then_inc(s.ginv_made, 1)
            dve.wait_ge(s.exp_made, 3)
            nc.vector.sem_inc(s.bank_free, BLK)

            def masks(g, head, part, slot_row, qs):
                for q in qs:
                    sl = q % 2
                    first = isinstance(g, int) and g == 0 and q < 2
                    if q % 2 == 1:
                        if q == 1:
                            dve.wait_ge(s1row_loaded[slot_row], row_loads(g, slot_row))
                        if not first:
                            dve.wait_ge(s.pos_made, NQ * g + q - 1)
                        nc.vector.tensor_scalar(cmp[:, sl, 1, :], s1row[:, slot_row, :],
                                                ns2[:, head, 2 * q + 1:2 * q + 2], MASK_ONE,
                                                ALU.is_gt, ALU.mult).then_inc(s.cmp_dve, 1)
                        dve.wait_ge(s.cmp_dve, NQ // 2 * g + q // 2 + 1)
                    dve.wait_ge(s.cmp_act, 3 * NQ // 2 * g + 3 * (q // 2) + 2 + q % 2)
                    if q >= 2:
                        dve.wait_ge(s.pos_used, (NQ - 1) * g + q - 1)
                    elif not first and q == 0:
                        dve.wait_ge(s.pos_used, (NQ - 1) * g)
                    elif not first:
                        dve.wait_ge(s.bank_ready, BLK * g)
                    a_ = adjT[:, 2 * q:2 * q + 2, bass.ds(part * BN, BN)].bitcast(U16)
                    nc.vector.tensor_tensor(pos[:, sl, :, :].bitcast(U16), a_, cmp[:, sl, :, :].bitcast(U16),
                                            ALU.bitwise_and).then_inc(s.pos_made, 1)
                    if q >= 2:
                        dve.wait_ge(s.neg_used, (NQ - 1) * g + q - 1)
                    elif not first and q == 0:
                        dve.wait_ge(s.neg_used, (NQ - 1) * g)
                    dve.wait_ge(s.pos_made, NQ * g + q + 1)
                    nc.vector.tensor_tensor(neg[:, sl, :, :].bitcast(U16), a_, pos[:, sl, :, :].bitcast(U16),
                                            ALU.bitwise_xor).then_inc(s.neg_made, 1)

            def evacuate(g, head, part):
                for k in range(BLK):
                    dve.wait_ge(s.mixA_made, BLK * g + k + 1)
                    nc.vector.scalar_tensor_tensor(out=mix[:, k, :], in0=ps[:, k, V2:2 * V2],
                                                   scalar=rowC[:, head, bass.ds(part * BLK + k, 1)],
                                                   in1=mix[:, k, :], op0=ALU.mult, op1=ALU.add)\
                        .then_inc(s.bank_free, 1)
                dve.wait_ge(s.bank_free, BLK * (g + 2))
                if not (isinstance(g, int) and g == 0):
                    dve.wait_ge(s.hout_made, g)
                nc.vector.tensor_tensor(den[:, 0, :], mix[:, :, DH], mix[:, :, V1 + DH], ALU.add)\
                    .then_inc(s.den_step, 1)
                dve.wait_ge(s.den_step, 2 * g + 4)
                nc.vector.reciprocal(den[:, 1, :], den[:, 0, :]).then_inc(s.den_step, 1)
                dve.wait_ge(s.den_step, 2 * g + 5)
                nc.vector.tensor_scalar(den[:, 2, :], den[:, 1, :], amax[:, bass.ds(head, 1)], None, ALU.mult)\
                    .then_inc(s.den_made, 1)

            masks(0, 0, 0, 0, range(0, NQ))
            masks(1, 0, 1, 1, (0, 1))
            evacuate(0, 0, 0)
            with dve.Fori(0, H - 1) as hd:
                for b in range(1, NB + 1):
                    g = hd * NB + b
                    h_, b_ = hd + b // NB, b % NB
                    masks(g, h_, b_, b % 2, range(2, NQ))
                    masks(g + 1, hd + (b + 1) // NB, (b + 1) % NB, (b + 1) % 2, (0, 1))
                    evacuate(g, h_, b_)
            for g in range(G - NB + 1, G):
                masks(g, H - 1, g % NB, g % 2, range(2, NQ))
                if g + 1 < G:
                    masks(g + 1, H - 1, (g + 1) % NB, (g + 1) % 2, (0, 1))
                evacuate(g, H - 1, g % NB)
            for k in range(KT):
                dve.wait_ge(s.wo_hi_made, k + 1)
                nc.vector.scalar_tensor_tensor(out=o_lo[:, k, :], in0=o_in[:, k, :], scalar=W_SCALE,
                                               in1=o_hi[:, k, :], op0=ALU.mult, op1=ALU.subtract)\
                    .then_inc(s.wo_split, 1)
            dve.wait_ge(s.b_loaded, DMA)
            for u in range(2):
                nc.vector.sem_inc(o_stored[u], DMA)
            with dve.Fori(0, NT // 2) as r:
                for u in range(2):
                    t = 2 * r + u
                    dve.wait_ge(s.hhi_made, t + 1)
                    nc.vector.scalar_tensor_tensor(out=hT_lo[:, u, :], in0=xT_ps, scalar=H_SCALE,
                                                   in1=hT_hi[:, u, :], op0=ALU.mult, op1=ALU.subtract)\
                        .then_inc(s.hlo_made, 1)
                    for n in range(2):
                        cs = slice(n * HALF, (n + 1) * HALF)
                        dve.wait_ge(s.o_written, 2 * t + n + 1)
                        nc.vector.scalar_tensor_tensor(out=zbuf[:, u, cs], in0=proj_ps[2 * u + n],
                                                       scalar=1.0 / (W_SCALE * H_SCALE), in1=b_row[:, cs],
                                                       op0=ALU.mult, op1=ALU.add).then_inc(s.z_made, 1)
                    dve.wait_ge(s.z_made, 2 * t + 2)
                    nc.vector.tensor_scalar(ebuf[:, u, :], zbuf[:, u, :], 0.0, None, ALU.min)\
                        .then_inc(s.e_in_made, 1)
                    dve.wait_ge(xres_loaded[u], (r + 1) * DMA)
                    nc.vector.scalar_tensor_tensor(out=zbuf[:, u, :], in0=zbuf[:, u, :], scalar=0.0,
                                                   in1=xres[:, u, :], op0=ALU.max, op1=ALU.add)\
                        .then_inc(s.y_made, 1)
                    dve.wait_ge(s.y_made, t + 1)
                    dve.wait_ge(s.e_made, t + 1)
                    dve.wait_ge(o_stored[u], (r + 1) * DMA)
                    nc.vector.scalar_tensor_tensor(out=ybuf[:, u, :], in0=ebuf[:, u, :], scalar=-1.0,
                                                   in1=zbuf[:, u, :], op0=ALU.add, op1=ALU.add)\
                        .then_inc(s.y2_made, 1)
                    dve.wait_ge(s.y2_made, t + 1)
                    for n in range(2):
                        nc.vector.bn_stats(bnst[:, n, :], ybuf[:, u, n * HALF:(n + 1) * HALF])\
                            .then_inc(s.bn_made, 1)
                    wait_alone(dve, "dve", s.bn_made, 2 * t + 2)
                    nc.vector.bn_aggr(mv[:, :], bnst[:, :, :]).then_inc(s.mv_made, 1)
                    dve.wait_ge(s.mv_made, 2 * t + 1)
                    nc.vector.tensor_scalar(mv[:, 1:2], mv[:, 1:2], EPS, None, ALU.add).then_inc(s.mv_made, 1)
                    dve.wait_ge(s.rstd_made, t + 1)
                    nc.vector.scalar_tensor_tensor(out=nmr[:, u, 0:1], in0=mv[:, 0:1], scalar=-1.0,
                                                   in1=rstd[:, u:u + 1], op0=ALU.mult, op1=ALU.mult)\
                        .then_inc(s.nmr_made, 1)

        @block.tensor
        def _(pe):
            pe.wait_ge(s.ident_made, 4)

            def transpose_rows(src, done):
                for k in range(KT):
                    last = nc.tensor.transpose(xT_ps[:, k * P:(k + 1) * P], src[:, k * P:(k + 1) * P],
                                               ident_f[:, :])
                last.then_inc(done, 1)

            def project(bank, lhs_hi, lhs_lo, r_hi, r_lo, n):
                cs = slice(n * HALF, (n + 1) * HALF)
                for k in range(KT):
                    hi, lo = lhs_hi[:, k * P:(k + 1) * P], lhs_lo[:, k * P:(k + 1) * P]
                    nc.tensor.matmul(proj_ps[bank], hi, r_hi[:, k, cs], start=(k == 0), stop=False)
                    nc.tensor.matmul(proj_ps[bank], hi, r_lo[:, k, cs], start=False, stop=False)
                    last = nc.tensor.matmul(proj_ps[bank], lo, r_hi[:, k, cs], start=False,
                                            stop=(k == KT - 1))
                return last

            with pe.Fori(0, NT // 2) as r:
                for u in range(2):
                    t = 2 * r + u
                    pe.wait_ge(x_loaded[u], (r + 1) * DMA)
                    transpose_rows(xin[:, u, :], s.xT_written)
                    pe.wait_ge(s.adj_fixed, t + 1)
                    for g in range(4):
                        for i in range(8):
                            j = 8 * g + i
                            last = nc.tensor.transpose(adjT_ps[g % 2][:, i, :],
                                                       adj_in[:, u, j * P:(j + 1) * P], ident_b[:, :])
                        last.then_inc(s.adjT_written, 1)
                        if g == 1:
                            pe.wait_ge(s.adjT_act, 2 * t + 1)
                        if g == 2:
                            pe.wait_ge(s.adjT_dve, 2 * t + 1)
                    pe.wait_ge(s.w_split, KT)
                    pe.wait_ge(s.xlo_made, t + 1)
                    for n in range(2):
                        project(2 * u + n, xT_hi[:, u, :], xT_lo[:, u, :], w_hi, w_lo, n)\
                            .then_inc(s.proj_written, 1)
                    pe.wait_ge(s.adjT_act, 2 * t + 2)
                    pe.wait_ge(s.adjT_dve, 2 * t + 2)
            pe.wait_ge(s.seq_reduced, 2 * NT + 2)
            for k in range(4):
                last = nc.tensor.transpose(ps[:, 0, k * P:(k + 1) * P],
                                           s1[:, 4 * k:4 * k + 4, :].rearrange("p h t -> p (h t)"),
                                           ident_f[:, :])
            last.then_inc(s.s1T_written, 1)
            pe.wait_ge(s.s1T_copied, 1)
            pe.wait_ge(s.seq_copied, 2 * NT)

            def mm(k, m, sl, jj, par, j, br, start, stop):
                return nc.tensor.matmul(ps[:, k, br * V2:(br + 1) * V2],
                                        m[:, sl, jj, k * P:(k + 1) * P].bitcast(F8),
                                        rhs[:, par, j, br, :], start=start, stop=stop,
                                        skip_group_check=True)

            with pe.Fori(0, H // 2) as hp:
                for par in range(2):
                    wait_alone(pe, "pe", s.rhs_step, RS * NB * (2 * hp + par + 1))
                    with pe.Fori(0, NB) as b:
                        g = (2 * hp + par) * NB + b
                        for q in range(NQ - 1):
                            sl = q % 2
                            wait_alone(pe, "pe", s.pos_made, NQ * g + q + 1)
                            for jj in range(2):
                                for k in range(BLK):
                                    if q == 0 and jj == 0:
                                        wait_alone(pe, "pe", s.bank_free, BLK * g + k + 1)
                                    last = mm(k, pos, sl, jj, par, 2 * q + jj, 0, q == 0 and jj == 0, False)
                            last.then_inc(s.pos_used, 1)
                            wait_alone(pe, "pe", s.neg_made, NQ * g + q + 1)
                            for jj in range(2):
                                for k in range(BLK):
                                    last = mm(k, neg, sl, jj, par, 2 * q + jj, 1, False, False)
                            last.then_inc(s.neg_used, 1)
                        q, sl = NQ - 1, (NQ - 1) % 2
                        wait_alone(pe, "pe", s.pos_made, NQ * g + q + 1)
                        wait_alone(pe, "pe", s.neg_made, NQ * g + q + 1)
                        for k in range(BLK):
                            for jj in range(2):
                                mm(k, pos, sl, jj, par, 2 * q + jj, 0, False, False)
                            for jj in range(2):
                                last = mm(k, neg, sl, jj, par, 2 * q + jj, 1, False, jj == 1)
                            last.then_inc(s.bank_ready, 1)
            pe.wait_ge(s.bank_free, BLK * (G + 1))
            pe.wait_ge(s.wo_split, KT)
            with pe.Fori(0, NT // 2) as r:
                for u in range(2):
                    t = 2 * r + u
                    pe.wait_ge(hin_loaded[u], (r + 1) * DMA)
                    transpose_rows(hin[:, u, :], s.hT_written)
                    pe.wait_ge(s.hlo_made, t + 1)
                    for n in range(2):
                        project(2 * u + n, hT_hi[:, u, :], hT_lo[:, u, :], o_hi, o_lo, n)\
                            .then_inc(s.o_written, 1)


_INS = ["x", "adj", "L0_gnn_W_seq", "L0_gnn_a1", "L0_gnn_a2", "L0_gnn_W_out", "L0_gnn_b_out"]


def kernel(**inputs):
    import numpy as _np
    import concourse.bacc as _bacc
    from concourse.bass_utils import run_bass_kernel_spmd as _run

    nc = _bacc.Bacc("TRN2", target_bir_lowering=False, num_devices=1)
    arrays, args = {}, []
    for name in _INS:
        a = _np.ascontiguousarray(inputs[name])
        arrays[f"in_{name}"] = a
        args.append(nc.dram_tensor(f"in_{name}", a.shape, mybir.dt.from_np(a.dtype), kind="ExternalInput").ap())
    out = nc.dram_tensor("out", (N, D), F32, kind="ExternalOutput").ap()
    build(nc, *args, out)
    r = _run(nc, [arrays], core_ids=[0])
    return r.results[0]["out"]
```

```python
import math
from contextlib import ExitStack

import concourse.bass as bass
from concourse import mybir

F32 = mybir.dt.float32
F16 = mybir.dt.float16
BF16 = mybir.dt.bfloat16
F8 = mybir.dt.float8e4
U8 = mybir.dt.uint8
I8 = mybir.dt.int8
U16 = mybir.dt.uint16
ALU = mybir.AluOpType
ACT = mybir.ActivationFunctionType
AX = mybir.AxisListType

P = 128
N, D, H = 4096, 1024, 16
DH = D // H
NT = N // P
KT = D // P
HALF = D // 2
HH = H // 2
BLK = 8
BN = BLK * P
NB = N // BN
G = H * NB
NQ = NT // 2
V1 = DH + 1
V2 = 2 * V1
CT = NT // NB
EPS = 1e-5
W_SCALE = 256.0
H_SCALE = 16.0
V_SCALE = 2.0 ** 15
MASK_ONE = 64.0
CMP_SLOTS = 4
SLOT = [q % 3 for q in range(NQ - 1)] + [1]
LAST_USE = [max(p - NQ for p in range(NQ + q) if SLOT[p % NQ] == SLOT[q]) for q in range(NQ)]
RS = 9
DMA = 16


def build(nc, x, adj, w_seq, a1, a2, w_out, b_out, out):
    seq_d = nc.dram_tensor("seq_d", (N, D), F32).ap()
    hid_d = nc.dram_tensor("hid_d", (N, D), F32).ap()
    wo_d = nc.dram_tensor("wo_d", (2, KT, P, D), F16).ap()
    s1_d = nc.dram_tensor("s1_d", (H * NT, P), F32).ap()

    x_t = x.rearrange("(t p) c -> t p c", p=P)
    adj_t = adj.rearrange("(t p) c -> t p c", p=P)
    out_t = out.rearrange("(t p) c -> t p c", p=P)
    seq_st = seq_d.rearrange("(t p) c -> t p c", p=P)
    hid_t = hid_d.rearrange("(t p) c -> t p c", p=P)
    seq_ld = seq_d.rearrange("(b t p) (h d) -> h b p t d", p=P, t=CT, d=DH)
    hid_st = hid_d.rearrange("(b t p) (h d) -> h b p t d", p=P, t=BLK, d=DH)
    s1_g = s1_d.rearrange("(g t) p -> g (t p)", t=BLK)

    ctx = ExitStack()
    with ctx:
        def sb(name, shape, dt, c=None):
            return (c or ctx).enter_context(nc.sbuf_tensor(name, shape, dt))

        def sem(name):
            return ctx.enter_context(nc.semaphore(name))

        ident_f = sb("ident_f", [P, P], F32)
        ph13 = ExitStack()
        adjT = sb("adjT", [P, NT, N], U8, ph13)
        s1 = sb("s1", [P, H, NT], F32, ph13)
        s2 = sb("s2", [P, H, NT], F32, ph13)
        stat = sb("stat", [P, 2, H], F32, ph13)
        stat_r = sb("stat_r", [P, 2, H], F32, ph13)
        ph1 = ExitStack()
        ident_b = sb("ident_b", [P, P], BF16, ph1)
        w_hi = sb("w_hi", [P, KT, D], F16, ph1)
        w_lo = sb("w_lo", [P, KT, D], F16, ph1)
        xin = sb("xin", [P, 2, D], F32, ph1)
        xT_hi = sb("xT_hi", [P, 2, D], F16, ph1)
        xT_lo = sb("xT_lo", [P, 2, D], F16, ph1)
        seq_o = sb("seq_o", [P, D], F32, ph1)
        prod = sb("prod", [P, HALF], F32, ph1)
        adj_in = sb("adj_in", [P, 2, N], BF16, ph1)
        a_row = sb("a_row", [P, 2, DH], F32, ph1)
        smax = sb("smax", [P, H, NT], F32, ph1)
        degree = sb("degree", [P, 2], F32, ph1)
        lonely = sb("lonely", [P, 1], F32, ph1)
        ph1.close()
        ph3 = ExitStack()
        ns2, rowA = s2, s1
        rowC = sb("rowC", [P, H, NT], F32, ph3)
        colB = sb("colB", [P, 2, H, NT], F32, ph3)
        rhs = sb("rhs", [P, 2, NT, 2, V2], F16, ph3)
        s1row = sb("s1row", [P, 2, BN], F32, ph3)
        cmp = sb("cmp", [P, CMP_SLOTS, 2, BN], U8, ph3)
        pos = sb("pos", [P, 3, 2, BN], U8, ph3)
        neg = sb("neg", [P, 3, 2, BN], U8, ph3)
        stage = sb("stage", [P, CT, DH], F32, ph3)
        vbuf = sb("vbuf", [P, CT, V1], F32, ph3)
        mix = sb("mix", [P, BLK, V2], F32, ph3)
        vcol = sb("vcol", [P, 2, CT], F32, ph3)
        den = sb("den", [P, 3, BLK], F32, ph3)
        amax = sb("amax", [P, H], F32, ph3)
        ginv = sb("ginv", [P, H], F32, ph3)
        ph3.close()
        tmpa = rhs[:, 0, 0:4 * H * NT // V2 // 2 + 2, :, :].rearrange("p a b c -> p (a b c)")[
            :, 0:4 * H * NT].bitcast(F32).rearrange("p (r h t) -> p r h t", r=2, t=NT)
        w_raw = adjT[:, NT - KT:NT, :].bitcast(F32)
        wo_raw = adjT[:, 0:4, 3 * N // 4:N].bitcast(F32)
        wo_part = [adjT[:, 4 + 2 * i:6 + 2 * i, 3 * N // 4:N].bitcast(F16) for i in range(2)]
        s1T = cmp[:, :, :, :].rearrange("p a b c -> p (a b c)")[:, 0:4 * 4 * P].bitcast(F32)\
            .rearrange("p (k c) -> p k c", k=4)
        ph13.close()
        ph4 = ExitStack()
        o_w = sb("o_w", [P, 2, KT, D], F16, ph4)
        o_hi, o_lo = o_w[:, 0, :, :], o_w[:, 1, :, :]
        hin = sb("hin", [P, 2, D], F32, ph4)
        xres = sb("xres", [P, 2, D], F32, ph4)
        b_row = sb("b_row", [P, D], F32, ph4)
        hT_hi = sb("hT_hi", [P, 2, D], F16, ph4)
        hT_lo = sb("hT_lo", [P, 2, D], F16, ph4)
        zbuf = sb("zbuf", [P, 2, D], F32, ph4)
        ebuf = sb("ebuf", [P, 2, D], F32, ph4)
        ybuf = sb("ybuf", [P, 2, D], F32, ph4)
        bnst = sb("bnst", [P, 2, 6], F32, ph4)
        mv = sb("mv", [P, 2], F32, ph4)
        nmr = sb("nmr", [P, 2, 2], F32, ph4)
        rstd = sb("rstd", [P, 2], F32, ph4)
        minus_half = sb("minus_half", [P, 1], F32, ph4)
        ph4.close()

        ps = ctx.enter_context(nc.psum_tensor("ps", [P, 8, HALF], F32))
        xT_ps = ps[:, 0:2, :].rearrange("p a c -> p (a c)")
        adjT_ps = [ps[:, 2 + b, :].bitcast(BF16).rearrange("p (g c) -> p g c", c=P) for b in range(2)]
        proj_ps = [ps[:, 4 + b, :] for b in range(4)]

        names = """ident_made a_loaded w_hi_made w_split
            degree_made lonely_made adj_fixed xT_written xhi_made xlo_made adjT_written adjT_act
            adjT_dve proj_written seq_copied seq_reduced prod_made score_made
            stat_made stat_reduced ginv_made expin_made exp_made s1T_written s1T_copied
            s1_stored cmp_act cmp_dve pos_made neg_made pos_used neg_used rhs_step
            bank_ready bank_free mixA_made parts_added den_made den_step hout_made hid_stored stage_loaded
            wo_read wo_step wo_stored wo_loaded b_loaded
            half_made hT_written hhi_made hlo_made o_written
            z_made e_in_made e_made y_made y2_made bn_made mv_made rstd_made nmr_made yn_made
            """.split()
        s = type("Sems", (), {n: sem(n) for n in names})
        x_loaded, adj_loaded, seq_stored, s1row_loaded, hin_loaded, \
            xres_loaded, o_stored = ([sem(f"{n}_{u}") for u in range(2)] for n in (
                "x_loaded", "adj_loaded", "seq_stored", "s1row_loaded", "hin_loaded", "xres_loaded", "o_stored"))
        w_loaded = [sem(f"w_loaded_{k}") for k in range(KT)]

        tally = {e: sem(e + "_tally") for e in ("sp", "act", "dve", "pe")}

        def wait_alone(eng, name, semaphore, value):
            eng.wait_ge(semaphore, value)
            eng.sem_inc(tally[name], 1)

        def row_loads(g, slot):
            return (g - slot) * (DMA // 2) + DMA

        block = ctx.enter_context(nc.Block())

        @block.sync
        def _(sp):
            sp.dma_start(a_row[:, 0, :], a1.partition_broadcast(P)).then_inc(s.a_loaded, DMA)
            sp.dma_start(a_row[:, 1, :], a2.partition_broadcast(P)).then_inc(s.a_loaded, DMA)
            for k in range(KT):
                sp.dma_start(w_raw[:, k, :], w_seq[k * P:(k + 1) * P, :]).then_inc(w_loaded[k], DMA)
                if k < 2:
                    sp.dma_start(xin[:, k, :], x_t[k, :, :]).then_inc(x_loaded[k], DMA)

            def load_x(r0, r1):
                with sp.Fori(r0, r1) as r:
                    for u in range(2):
                        sp.wait_ge(s.xT_written, 2 * r + u - 1)
                        sp.dma_start(xin[:, u, :], x_t[2 * r + u, :, :]).then_inc(x_loaded[u], DMA)

            load_x(1, 3 * NT // 8)
            sp.wait_ge(s.wo_stored, 2 * KT * DMA)
            load_x(3 * NT // 8, NT // 2)
            sp.wait_ge(s.s1T_copied, 1)
            sp.dma_start(s1_d.rearrange("(k r) c -> r k c", r=P), s1T).then_inc(s.s1_stored, DMA)
            for n in range(2):
                sp.wait_ge(seq_stored[n], (NT + 1) * DMA)

            def load_stage(head, part):
                sp.dma_start(stage[:, :, :], seq_ld[head, part, :, :, :]).then_inc(s.stage_loaded, DMA)

            sp.wait_ge(s.s1T_written, 1)
            load_stage(0, 0)
            sp.wait_ge(s.s1_stored, DMA)

            def load_row(g, slot):
                sp.dma_start(s1row[:, slot, :], s1_g[g, :].partition_broadcast(P)).then_inc(s1row_loaded[slot], DMA)

            load_row(0, 0)
            load_row(1, 1)
            for c in range(1, NB + 1):
                sp.wait_ge(s.rhs_step, RS * c)
                load_stage(c // NB, c % NB)

            def store_hidden(head, part, g):
                sp.wait_ge(s.hout_made, g + 1)
                sp.dma_start(hid_st[head, part, :, :, :], mix[:, :, 0:DH]).then_inc(s.hid_stored, DMA)

            def next_row(g, slot):
                wait_alone(sp, "sp", s.cmp_act, (g + 1) * (NT * 3 // 4))
                wait_alone(sp, "sp", s.cmp_dve, (g + 1) * (NT // 4))
                load_row(g + 2, slot)

            with sp.Fori(0, H - 2) as hd:
                for b in range(NB):
                    g, c = hd * NB + b, b + 5
                    store_hidden(hd, b, g)
                    next_row(g, b % 2)
                    sp.wait_ge(s.rhs_step, RS * (g + 5))
                    load_stage(hd + c // NB, c % NB)
            for g in range(G - 2 * NB, G - 1):
                store_hidden(g // NB, g % NB, g)
                if g + 2 < G:
                    next_row(g, g % 2)
                if g + 5 < G:
                    sp.wait_ge(s.rhs_step, RS * (g + 5))
                    load_stage((g + 5) // NB, (g + 5) % NB)
            sp.wait_ge(s.neg_made, NQ * G)
            sp.dma_start(o_w[:, :, :, :], wo_d.rearrange("i k p c -> p i k c")).then_inc(s.wo_loaded, DMA)
            sp.dma_start(b_row[:, :], b_out.partition_broadcast(P)).then_inc(s.b_loaded, DMA)

            def load_out(t, u):
                sp.dma_start(hin[:, u, :], hid_t[t, :, :]).then_inc(hin_loaded[u], DMA)
                sp.dma_start(xres[:, u, :], x_t[t, :, :]).then_inc(xres_loaded[u], DMA)

            load_out(0, 0)
            load_out(1, 1)
            store_hidden(H - 1, NB - 1, G - 1)
            sp.wait_ge(s.hid_stored, G * DMA)
            with sp.Fori(1, NT // 2) as r:
                for u in range(2):
                    sp.wait_ge(s.hT_written, 2 * r + u - 1)
                    sp.wait_ge(s.y_made, 2 * r + u - 1)
                    load_out(2 * r + u, u)
            for u in range(2):
                sp.wait_ge(o_stored[u], (NT // 2 + 1) * DMA)

        @block.gpsimd
        def _(pool):
            for i, m in enumerate((ident_b, ident_f)):
                nc.gpsimd.memset(m[:, :], 0.0).then_inc(s.ident_made, 1)
                pool.wait_ge(s.ident_made, 2 * i + 1)
                nc.gpsimd.affine_select(out=m[:, :], in_=m[:, :], compare_op=ALU.not_equal, fill=1.0,
                                        base=0, pattern=[[-1, P]], channel_multiplier=1)\
                    .then_inc(s.ident_made, 1)
            def load_adj(r0, r1):
                with pool.Fori(r0, r1) as r:
                    for u in range(2):
                        pool.wait_ge(s.adjT_written, 4 * (2 * r + u - 1))
                        pool.dma_start(adj_in[:, u, :], adj_t[2 * r + u, :, :]).then_inc(adj_loaded[u], DMA)

            for u in range(2):
                pool.dma_start(adj_in[:, u, :], adj_t[u, :, :]).then_inc(adj_loaded[u], DMA)
            for k in range(KT):
                pool.dma_start(wo_raw, w_out[k * P:(k + 1) * P, :].rearrange("p (a c) -> p a c", a=4))\
                    .then_inc(s.wo_read, DMA)
                load_adj(k + 1, k + 2)
                pool.wait_ge(s.wo_read, (k + 1) * DMA)
                nc.gpsimd.tensor_scalar(wo_raw, wo_raw, W_SCALE, None, ALU.mult).then_inc(s.wo_step, 1)
                pool.wait_ge(s.wo_step, 3 * k + 1)
                if k:
                    pool.wait_ge(s.wo_stored, 2 * k * DMA)
                hi, lo = (w.rearrange("p i (a c) -> p i a c", a=2) for w in wo_part)
                whole = wo_raw.rearrange("p (i a) c -> p i a c", a=2)
                nc.gpsimd.tensor_copy(hi, whole).then_inc(s.wo_step, 1)
                pool.wait_ge(s.wo_step, 3 * k + 2)
                nc.gpsimd.tensor_tensor(lo, whole, hi, ALU.subtract).then_inc(s.wo_step, 1)
                pool.wait_ge(s.wo_step, 3 * k + 3)
                for i, part in enumerate(wo_part):
                    pool.dma_start(wo_d[i, k, :, :].rearrange("p (a c) -> p a c", a=2), part)\
                        .then_inc(s.wo_stored, DMA)
            load_adj(KT + 1, NT // 2)
            pool.wait_ge(s.stat_made, 2)
            nc.gpsimd.partition_all_reduce(stat_r[:, :, :], stat[:, :, :], P, bass.bass_isa.ReduceOp.max)\
                .then_inc(s.stat_reduced, 1)
            pool.wait_ge(s.exp_made, 3)
            pool.wait_ge(s.ginv_made, 2)

            def chunk(c, head, part, par):
                pool.wait_ge(s.stage_loaded, (c + 1) * DMA)
                if not isinstance(c, int):
                    pool.wait_ge(s.bank_ready, BLK * NB * (head - 1))
                ts = bass.ds(part * CT, CT)
                nc.gpsimd.tensor_tensor(vcol[:, :, :], colB[:, :, head, ts],
                                        ginv[:, bass.ds(head, 1)].unsqueeze(2).to_broadcast([P, 2, CT]),
                                        ALU.mult).then_inc(s.rhs_step, 1)
                pool.wait_ge(s.rhs_step, RS * c + 1)
                for br in range(2):
                    n = RS * c + 1 + 4 * br
                    nc.gpsimd.tensor_tensor(vbuf[:, :, 0:DH], stage[:, :, :],
                                            vcol[:, br, :].unsqueeze(2).to_broadcast([P, CT, DH]),
                                            ALU.mult).then_inc(s.rhs_step, 1)
                    nc.gpsimd.tensor_copy(vbuf[:, :, DH], colB[:, br, head, ts]).then_inc(s.rhs_step, 1)
                    pool.wait_ge(s.rhs_step, n + 2)
                    nc.gpsimd.tensor_copy(rhs[:, par, ts, br, 0:V1], vbuf[:, :, :]).then_inc(s.rhs_step, 1)
                    pool.wait_ge(s.rhs_step, n + 3)
                    nc.gpsimd.tensor_tensor(rhs[:, par, ts, br, V1:V2], vbuf[:, :, :],
                                            rhs[:, par, ts, br, 0:V1], ALU.subtract)\
                        .then_inc(s.rhs_step, 1)
                    pool.wait_ge(s.rhs_step, n + 4)

            for c in range(NB):
                chunk(c, 0, c, 0)

            def combine(g):
                pool.wait_ge(s.bank_free, BLK * (g + 2))
                both = mix[:, :, 0:DH]
                nc.gpsimd.tensor_tensor(both, both, mix[:, :, V1:V1 + DH], ALU.add)\
                    .then_inc(s.parts_added, 1)
                pool.wait_ge(s.parts_added, g + 1)
                pool.wait_ge(s.den_made, g + 1)
                nc.gpsimd.tensor_tensor(both, both,
                                        den[:, 2, :].unsqueeze(2).to_broadcast([P, BLK, DH]), ALU.mult)\
                    .then_inc(s.hout_made, 1)

            for b in range(NB):
                chunk(b + NB, 1, b, 1)
                combine(b)
            with pool.Fori(1, H - 1) as hd:
                par = (hd + 1) % 2
                for b in range(NB):
                    chunk((hd + 1) * NB + b, hd + 1, b, par)
                    combine(hd * NB + b)
            for b in range(NB):
                combine((H - 1) * NB + b)
            pool.wait_ge(s.hid_stored, G * DMA)
            nc.gpsimd.memset(minus_half[:, :], -0.5).then_inc(s.half_made, 1)
            pool.wait_ge(s.half_made, 1)
            with pool.Fori(0, NT // 2) as r:
                for u in range(2):
                    t = 2 * r + u
                    pool.wait_ge(s.mv_made, 2 * t + 2)
                    nc.gpsimd.tensor_tensor(rstd[:, u:u + 1], mv[:, 1:2], minus_half[:, :], ALU.pow)\
                        .then_inc(s.rstd_made, 1)

        @block.scalar
        def _(act):
            for k in range(KT):
                act.wait_ge(w_loaded[k], DMA)
                nc.scalar.activation(w_hi[:, k, :], w_raw[:, k, :], ACT.Copy, scale=W_SCALE)\
                    .then_inc(s.w_hi_made, 1)

            def degrees(t, r, u):
                act.wait_ge(adj_loaded[u], (r + 1) * DMA)
                nc.scalar.activation(adj_in[:, u, :], adj_in[:, u, :], ACT.Copy,
                                     accum_out=degree[:, u:u + 1]).then_inc(s.degree_made, 1)

            def x_high(t, u):
                act.wait_ge(s.xT_written, t + 1)
                nc.scalar.activation(xT_hi[:, u, :], xT_ps, ACT.Copy).then_inc(s.xhi_made, 1)

            def adj_copy(t, g):
                act.wait_ge(s.adjT_written, 4 * t + g + 1)
                nc.scalar.activation(adjT[:, 8 * g:8 * g + 8, bass.ds(t * P, P)], adjT_ps[0],
                                     ACT.Copy).then_inc(s.adjT_act, 1)

            def seq_copy(t, u, n):
                act.wait_ge(s.proj_written, 2 * t + n + 1)
                act.wait_ge(s.seq_reduced, 2 * t + n + 1)
                act.wait_ge(seq_stored[n], (t + 1) * DMA)
                nc.scalar.activation(seq_o[:, n * HALF:(n + 1) * HALF], proj_ps[2 * u + n],
                                     ACT.Copy, scale=1.0 / W_SCALE).then_inc(s.seq_copied, 1)
                act.wait_ge(s.seq_copied, 2 * t + n + 1)
                act.dma_start(seq_st[t, :, n * HALF:(n + 1) * HALF],
                              seq_o[:, n * HALF:(n + 1) * HALF]).then_inc(seq_stored[n], DMA)

            def project_tile(t, r, u, more):
                adj_copy(t, 0)
                seq_copy(t, u, 0)
                adj_copy(t, 2)
                if more:
                    x_high(t + 1, 1 - u)
                    degrees(t + 1, r + u, 1 - u)
                seq_copy(t, u, 1)

            x_high(0, 0)
            degrees(0, 0, 0)
            with act.Fori(0, NT // 2 - 1) as r:
                for u in range(2):
                    project_tile(2 * r + u, r, u, True)
            for u in range(2):
                project_tile(NT - 2 + u, NT // 2 - 1, u, u == 0)
            act.wait_ge(s.s1T_written, 1)
            for n in range(2):
                act.wait_ge(seq_stored[n], (NT + 1) * DMA)
            nc.scalar.activation(s1T, ps[:, 0, :].rearrange("p (k c) -> p k c", k=4), ACT.Copy)\
                .then_inc(s.s1T_copied, 1)
            act.wait_ge(s.expin_made, 2)
            nc.scalar.activation(rowA[:, :, :], rowA[:, :, :], ACT.Exp).then_inc(s.exp_made, 1)
            nc.scalar.activation(rowC[:, :, :], rowC[:, :, :], ACT.Exp).then_inc(s.exp_made, 1)
            act.wait_ge(s.expin_made, 4)
            nc.scalar.activation(colB[:, :, :, :], colB[:, :, :, :], ACT.Exp).then_inc(s.exp_made, 1)
            act.wait_ge(s.s1_stored, DMA)

            def compare(slot_row, head, j, slot, jj):
                nc.scalar.activation(cmp[:, slot, jj, :].bitcast(I8), s1row[:, slot_row, :], ACT.Sign,
                                     scale=-1.0, bias=ns2[:, head, j:j + 1]).then_inc(s.cmp_act, 1)

            def pairs(g, head, slot_row, qs):
                for q in qs:
                    if q == 0:
                        act.wait_ge(s1row_loaded[slot_row], row_loads(g, slot_row))
                    if not (isinstance(g, int) and g == 0 and q < CMP_SLOTS):
                        wait_alone(act, "act", s.pos_made, NQ * g + q - CMP_SLOTS + 1)
                    compare(slot_row, head, 2 * q, q % CMP_SLOTS, 0)
                    if q % 2 == 0:
                        compare(slot_row, head, 2 * q + 1, q % CMP_SLOTS, 1)

            def evacuate(g, head, part):
                if not isinstance(g, int) or g > 0:
                    act.wait_ge(s.hid_stored, g * DMA)
                for k in range(BLK):
                    act.wait_ge(s.bank_ready, BLK * g + k + 1)
                    nc.scalar.activation(mix[:, k, :], ps[:, k, 0:V2], ACT.Copy,
                                         scale=rowA[:, head, bass.ds(part * BLK + k, 1)])\
                        .then_inc(s.mixA_made, 1)

            act.wait_ge(s.exp_made, 3)
            act.wait_ge(s.ginv_made, 1)
            pairs(0, 0, 0, (0, 1))
            pairs(0, 0, 0, range(2, NQ))
            pairs(1, 0, 1, (0, 1))
            evacuate(0, 0, 0)
            with act.Fori(0, H - 1) as hd:
                for b in range(1, NB + 1):
                    g = hd * NB + b
                    h_, b_ = hd + b // NB, b % NB
                    pairs(g, h_, b % 2, range(2, NQ))
                    pairs(g + 1, hd + (b + 1) // NB, (b + 1) % 2, (0, 1))
                    evacuate(g, h_, b_)
            for g in range(G - NB + 1, G):
                pairs(g, H - 1, g % 2, range(2, NQ))
                if g + 1 < G:
                    pairs(g + 1, H - 1, (g + 1) % 2, (0, 1))
                evacuate(g, H - 1, g % NB)
            def hidden_high(t, u):
                act.wait_ge(s.hT_written, t + 1)
                nc.scalar.activation(hT_hi[:, u, :], xT_ps, ACT.Copy, scale=H_SCALE).then_inc(s.hhi_made, 1)

            def output_tile(t, u, more):
                if more:
                    hidden_high(t + 1, 1 - u)
                act.wait_ge(s.e_in_made, t + 1)
                nc.scalar.activation(ebuf[:, u, :], ebuf[:, u, :], ACT.Exp).then_inc(s.e_made, 1)
                act.wait_ge(s.nmr_made, t + 1)
                nc.scalar.activation(ybuf[:, u, :], ybuf[:, u, :], ACT.Identity,
                                     scale=rstd[:, u:u + 1], bias=nmr[:, u, 0:1]).then_inc(s.yn_made, 1)
                act.wait_ge(s.yn_made, t + 1)
                act.dma_start(out_t[t, :, :], ybuf[:, u, :]).then_inc(o_stored[u], DMA)

            hidden_high(0, 0)
            with act.Fori(0, NT // 2 - 1) as r:
                for u in range(2):
                    output_tile(2 * r + u, u, True)
            for u in range(2):
                output_tile(NT - 2 + u, u, u == 0)

        @block.vector
        def _(dve):
            nc.vector.sem_inc(s.seq_reduced, 2)
            for n in range(2):
                nc.vector.sem_inc(seq_stored[n], DMA)
            for k in range(KT):
                dve.wait_ge(s.w_hi_made, k + 1)
                nc.vector.scalar_tensor_tensor(out=w_lo[:, k, :], in0=w_raw[:, k, :], scalar=W_SCALE,
                                               in1=w_hi[:, k, :], op0=ALU.mult, op1=ALU.subtract)\
                    .then_inc(s.w_split, 1)
            dve.wait_ge(s.a_loaded, 2 * DMA)

            def fix_adj(t, u):
                dve.wait_ge(s.degree_made, t + 1)
                nc.vector.tensor_scalar(lonely[:, :], degree[:, u:u + 1], 0.0, None, ALU.is_equal)\
                    .then_inc(s.lonely_made, 1)
                dve.wait_ge(s.lonely_made, t + 1)
                nc.vector.tensor_scalar(adj_in[:, u, :], adj_in[:, u, :], lonely[:, 0:1], MASK_ONE,
                                        ALU.max, ALU.mult).then_inc(s.adj_fixed, 1)

            def x_low(t, u):
                dve.wait_ge(s.xhi_made, t + 1)
                nc.vector.tensor_tensor(xT_lo[:, u, :], xT_ps, xT_hi[:, u, :], ALU.subtract)\
                    .then_inc(s.xlo_made, 1)

            def adj_copy(t, g):
                dve.wait_ge(s.adjT_written, 4 * t + g + 1)
                nc.vector.tensor_copy(adjT[:, 8 * g:8 * g + 8, bass.ds(t * P, P)], adjT_ps[1])\
                    .then_inc(s.adjT_dve, 1)

            def scores(t, n):
                dve.wait_ge(s.seq_copied, 2 * t + n + 1)
                half = seq_o[:, n * HALF:(n + 1) * HALF].rearrange("p (h d) -> p h d", d=DH)
                pr = prod[:, :].rearrange("p (h d) -> p h d", d=DH)
                hs = slice(n * HH, (n + 1) * HH)
                for v, dst in ((0, s1), (1, s2)):
                    i = 4 * t + 2 * n + v
                    nc.vector.tensor_tensor(pr, half, a_row[:, v, :].unsqueeze(1)
                                            .to_broadcast([P, HH, DH]), ALU.mult).then_inc(s.prod_made, 1)
                    dve.wait_ge(s.prod_made, i + 1)
                    nc.vector.tensor_reduce(dst[:, hs, bass.ds(t, 1)].rearrange("p h o -> p (h o)"),
                                            pr, AX.X, ALU.add).then_inc(s.score_made, 1)
                    dve.wait_ge(s.score_made, i + 1)
                nc.vector.tensor_reduce(smax[:, hs, bass.ds(t, 1)].rearrange("p h o -> p (h o)"),
                                        half, AX.X, ALU.max, apply_absolute_value=True)\
                    .then_inc(s.seq_reduced, 1)

            def project_tile(t, u, more):
                adj_copy(t, 1)
                scores(t, 0)
                adj_copy(t, 3)
                if more:
                    x_low(t + 1, 1 - u)
                    fix_adj(t + 1, 1 - u)
                scores(t, 1)

            x_low(0, 0)
            fix_adj(0, 0)
            with dve.Fori(0, NT // 2 - 1) as r:
                for u in range(2):
                    project_tile(2 * r + u, u, True)
            for u in range(2):
                project_tile(NT - 2 + u, u, u == 0)
            dve.wait_ge(s.seq_reduced, 2 * NT + 2)
            dve.wait_ge(s.score_made, 4 * NT)
            nc.vector.tensor_reduce(stat[:, 0, :], s2[:, :, :], AX.X, ALU.max).then_inc(s.stat_made, 1)
            nc.vector.tensor_reduce(stat[:, 1, :], smax[:, :, :], AX.X, ALU.max).then_inc(s.stat_made, 1)
            dve.wait_ge(s.stat_reduced, 1)
            dve.wait_ge(s.s1T_written, 1)
            for n in range(2):
                dve.wait_ge(seq_stored[n], (NT + 1) * DMA)
            top = stat_r[:, 0, :].unsqueeze(2).to_broadcast([P, H, NT])
            nc.vector.tensor_scalar(amax[:, :], stat_r[:, 1, :], 1e-30, None, ALU.max).then_inc(s.den_step, 1)
            nc.vector.tensor_tensor(tmpa[:, 0, :, :], s1[:, :, :], top, ALU.add).then_inc(s.den_step, 1)
            nc.vector.tensor_tensor(tmpa[:, 1, :, :], s2[:, :, :], top, ALU.subtract).then_inc(s.den_step, 1)
            dve.wait_ge(s.den_step, 3)
            nc.vector.tensor_scalar(rowA[:, :, :], tmpa[:, 0, :, :], 0.8, 0.0, ALU.mult, ALU.min)\
                .then_inc(s.expin_made, 1)
            nc.vector.tensor_scalar(rowC[:, :, :], tmpa[:, 0, :, :], -0.8, 0.0, ALU.mult, ALU.min)\
                .then_inc(s.expin_made, 1)
            nc.vector.tensor_scalar(colB[:, 0, :, :], tmpa[:, 1, :, :], math.log(V_SCALE), None, ALU.add)\
                .then_inc(s.expin_made, 1)
            nc.vector.tensor_scalar(colB[:, 1, :, :], tmpa[:, 1, :, :], 0.2, math.log(V_SCALE),
                                    ALU.mult, ALU.add).then_inc(s.expin_made, 1)
            nc.vector.tensor_scalar(ns2[:, :, :], s2[:, :, :], -1.0, None, ALU.mult).then_inc(s.ginv_made, 1)
            nc.vector.reciprocal(ginv[:, :], amax[:, :]).then_inc(s.ginv_made, 1)
            dve.wait_ge(s.exp_made, 3)
            nc.vector.sem_inc(s.bank_free, BLK)

            def masks(g, head, part, slot_row, qs):
                for q in qs:
                    cs, sl = q % CMP_SLOTS, SLOT[q]
                    start = isinstance(g, int) and g == 0
                    if q % 2 == 1:
                        if q == 1:
                            dve.wait_ge(s1row_loaded[slot_row], row_loads(g, slot_row))
                        if not (start and q < CMP_SLOTS):
                            dve.wait_ge(s.pos_made, NQ * g + q - CMP_SLOTS + 1)
                        nc.vector.tensor_scalar(cmp[:, cs, 1, :], s1row[:, slot_row, :],
                                                ns2[:, head, 2 * q + 1:2 * q + 2], MASK_ONE,
                                                ALU.is_gt, ALU.mult).then_inc(s.cmp_dve, 1)
                        dve.wait_ge(s.cmp_dve, NQ // 2 * g + q // 2 + 1)
                    dve.wait_ge(s.cmp_act, 3 * NQ // 2 * g + 3 * (q // 2) + 2 + q % 2)
                    last = LAST_USE[q]
                    if last == -1:
                        if not start:
                            dve.wait_ge(s.bank_ready, BLK * g)
                    elif not (start and last < 0):
                        dve.wait_ge(s.pos_used, (NQ - 1) * g + last + 1 + (last < 0))
                    a_ = adjT[:, 2 * q:2 * q + 2, bass.ds(part * BN, BN)].bitcast(U16)
                    nc.vector.tensor_tensor(pos[:, sl, :, :].bitcast(U16), a_, cmp[:, cs, :, :].bitcast(U16),
                                            ALU.bitwise_and).then_inc(s.pos_made, 1)
                    if last != -1 and not (start and last < 0):
                        dve.wait_ge(s.neg_used, (NQ - 1) * g + last + 1 + (last < 0))
                    dve.wait_ge(s.pos_made, NQ * g + q + 1)
                    nc.vector.tensor_tensor(neg[:, sl, :, :].bitcast(U16), a_, pos[:, sl, :, :].bitcast(U16),
                                            ALU.bitwise_xor).then_inc(s.neg_made, 1)

            def evacuate(g, head, part):
                for k in range(BLK):
                    dve.wait_ge(s.mixA_made, BLK * g + k + 1)
                    nc.vector.scalar_tensor_tensor(out=mix[:, k, :], in0=ps[:, k, V2:2 * V2],
                                                   scalar=rowC[:, head, bass.ds(part * BLK + k, 1)],
                                                   in1=mix[:, k, :], op0=ALU.mult, op1=ALU.add)\
                        .then_inc(s.bank_free, 1)
                dve.wait_ge(s.bank_free, BLK * (g + 2))
                if not (isinstance(g, int) and g == 0):
                    dve.wait_ge(s.hout_made, g)
                nc.vector.tensor_tensor(den[:, 0, :], mix[:, :, DH], mix[:, :, V1 + DH], ALU.add)\
                    .then_inc(s.den_step, 1)
                dve.wait_ge(s.den_step, 2 * g + 4)
                nc.vector.reciprocal(den[:, 1, :], den[:, 0, :]).then_inc(s.den_step, 1)
                dve.wait_ge(s.den_step, 2 * g + 5)
                nc.vector.tensor_scalar(den[:, 2, :], den[:, 1, :], amax[:, bass.ds(head, 1)], None, ALU.mult)\
                    .then_inc(s.den_made, 1)

            masks(0, 0, 0, 0, range(0, NQ))
            masks(1, 0, 1, 1, (0, 1))
            evacuate(0, 0, 0)
            with dve.Fori(0, H - 1) as hd:
                for b in range(1, NB + 1):
                    g = hd * NB + b
                    h_, b_ = hd + b // NB, b % NB
                    masks(g, h_, b_, b % 2, range(2, NQ))
                    masks(g + 1, hd + (b + 1) // NB, (b + 1) % NB, (b + 1) % 2, (0, 1))
                    evacuate(g, h_, b_)
            for g in range(G - NB + 1, G):
                masks(g, H - 1, g % NB, g % 2, range(2, NQ))
                if g + 1 < G:
                    masks(g + 1, H - 1, (g + 1) % NB, (g + 1) % 2, (0, 1))
                evacuate(g, H - 1, g % NB)
            dve.wait_ge(s.b_loaded, DMA)
            for u in range(2):
                nc.vector.sem_inc(o_stored[u], DMA)

            def hidden_low(t, u):
                dve.wait_ge(s.hhi_made, t + 1)
                nc.vector.scalar_tensor_tensor(out=hT_lo[:, u, :], in0=xT_ps, scalar=H_SCALE,
                                               in1=hT_hi[:, u, :], op0=ALU.mult, op1=ALU.subtract)\
                    .then_inc(s.hlo_made, 1)

            def output_tile(t, r, u, more):
                if more:
                    hidden_low(t + 1, 1 - u)
                for n in range(2):
                    cs = slice(n * HALF, (n + 1) * HALF)
                    dve.wait_ge(s.o_written, 2 * t + n + 1)
                    nc.vector.scalar_tensor_tensor(out=zbuf[:, u, cs], in0=proj_ps[2 * u + n],
                                                   scalar=1.0 / (W_SCALE * H_SCALE), in1=b_row[:, cs],
                                                   op0=ALU.mult, op1=ALU.add).then_inc(s.z_made, 1)
                dve.wait_ge(s.z_made, 2 * t + 2)
                nc.vector.tensor_scalar(ebuf[:, u, :], zbuf[:, u, :], 0.0, None, ALU.min)\
                    .then_inc(s.e_in_made, 1)
                dve.wait_ge(s.e_in_made, t + 1)
                dve.wait_ge(xres_loaded[u], (r + 1) * DMA)
                nc.vector.scalar_tensor_tensor(out=zbuf[:, u, :], in0=zbuf[:, u, :], scalar=0.0,
                                               in1=xres[:, u, :], op0=ALU.max, op1=ALU.add)\
                    .then_inc(s.y_made, 1)
                dve.wait_ge(s.y_made, t + 1)
                dve.wait_ge(s.e_made, t + 1)
                dve.wait_ge(o_stored[u], (r + 1) * DMA)
                nc.vector.scalar_tensor_tensor(out=ybuf[:, u, :], in0=ebuf[:, u, :], scalar=-1.0,
                                               in1=zbuf[:, u, :], op0=ALU.add, op1=ALU.add)\
                    .then_inc(s.y2_made, 1)
                dve.wait_ge(s.y2_made, t + 1)
                for n in range(2):
                    nc.vector.bn_stats(bnst[:, n, :], ybuf[:, u, n * HALF:(n + 1) * HALF])\
                        .then_inc(s.bn_made, 1)
                wait_alone(dve, "dve", s.bn_made, 2 * t + 2)
                nc.vector.bn_aggr(mv[:, :], bnst[:, :, :]).then_inc(s.mv_made, 1)
                dve.wait_ge(s.mv_made, 2 * t + 1)
                nc.vector.tensor_scalar(mv[:, 1:2], mv[:, 1:2], EPS, None, ALU.add).then_inc(s.mv_made, 1)
                dve.wait_ge(s.rstd_made, t + 1)
                nc.vector.scalar_tensor_tensor(out=nmr[:, u, 0:1], in0=mv[:, 0:1], scalar=-1.0,
                                               in1=rstd[:, u:u + 1], op0=ALU.mult, op1=ALU.mult)\
                    .then_inc(s.nmr_made, 1)

            hidden_low(0, 0)
            with dve.Fori(0, NT // 2 - 1) as r:
                for u in range(2):
                    output_tile(2 * r + u, r, u, True)
            for u in range(2):
                output_tile(NT - 2 + u, NT // 2 - 1, u, u == 0)

        @block.tensor
        def _(pe):
            pe.wait_ge(s.ident_made, 4)

            def transpose_rows(src, done):
                for k in range(KT):
                    last = nc.tensor.transpose(xT_ps[:, k * P:(k + 1) * P], src[:, k * P:(k + 1) * P],
                                               ident_f[:, :])
                last.then_inc(done, 1)

            def project(bank, lhs_hi, lhs_lo, r_hi, r_lo, n):
                cs = slice(n * HALF, (n + 1) * HALF)
                for k in range(KT):
                    hi, lo = lhs_hi[:, k * P:(k + 1) * P], lhs_lo[:, k * P:(k + 1) * P]
                    nc.tensor.matmul(proj_ps[bank], hi, r_hi[:, k, cs], start=(k == 0), stop=False)
                    nc.tensor.matmul(proj_ps[bank], hi, r_lo[:, k, cs], start=False, stop=False)
                    last = nc.tensor.matmul(proj_ps[bank], lo, r_hi[:, k, cs], start=False,
                                            stop=(k == KT - 1))
                return last

            def transpose_x(t, r, u):
                pe.wait_ge(x_loaded[u], (r + 1) * DMA)
                transpose_rows(xin[:, u, :], s.xT_written)

            def transpose_adj(t, u, g):
                for i in range(8):
                    j = 8 * g + i
                    last = nc.tensor.transpose(adjT_ps[g % 2][:, i, :],
                                               adj_in[:, u, j * P:(j + 1) * P], ident_b[:, :])
                last.then_inc(s.adjT_written, 1)

            def project_tile(t, r, u, more):
                pe.wait_ge(s.adj_fixed, t + 1)
                pe.wait_ge(s.xlo_made, t + 1)
                transpose_adj(t, u, 0)
                transpose_adj(t, u, 1)
                project(2 * u, xT_hi[:, u, :], xT_lo[:, u, :], w_hi, w_lo, 0).then_inc(s.proj_written, 1)
                pe.wait_ge(s.adjT_act, 2 * t + 1)
                transpose_adj(t, u, 2)
                pe.wait_ge(s.adjT_dve, 2 * t + 1)
                transpose_adj(t, u, 3)
                if more:
                    transpose_x(t + 1, r + u, 1 - u)
                project(2 * u + 1, xT_hi[:, u, :], xT_lo[:, u, :], w_hi, w_lo, 1).then_inc(s.proj_written, 1)

            transpose_x(0, 0, 0)
            pe.wait_ge(s.w_split, KT)
            with pe.Fori(0, NT // 2 - 1) as r:
                for u in range(2):
                    project_tile(2 * r + u, r, u, True)
            for u in range(2):
                project_tile(NT - 2 + u, NT // 2 - 1, u, u == 0)
            pe.wait_ge(s.seq_reduced, 2 * NT + 2)
            for k in range(4):
                last = nc.tensor.transpose(ps[:, 0, k * P:(k + 1) * P],
                                           s1[:, 4 * k:4 * k + 4, :].rearrange("p h t -> p (h t)"),
                                           ident_f[:, :])
            last.then_inc(s.s1T_written, 1)
            pe.wait_ge(s.s1T_copied, 1)
            pe.wait_ge(s.seq_copied, 2 * NT)

            def mm(k, m, sl, jj, par, j, br, start, stop):
                return nc.tensor.matmul(ps[:, k, br * V2:(br + 1) * V2],
                                        m[:, sl, jj, k * P:(k + 1) * P].bitcast(F8),
                                        rhs[:, par, j, br, :], start=start, stop=stop,
                                        skip_group_check=True)

            with pe.Fori(0, H // 2) as hp:
                for par in range(2):
                    with pe.Fori(0, NB) as b:
                        g = (2 * hp + par) * NB + b
                        for q in range(NQ - 1):
                            sl = SLOT[q]
                            if q % (NQ // NB) == 0:
                                wait_alone(pe, "pe", s.rhs_step,
                                           RS * (NB * (2 * hp + par) + q * NB // NQ + 1))
                            wait_alone(pe, "pe", s.pos_made, NQ * g + q + 1)
                            for jj in range(2):
                                for k in range(BLK):
                                    if q == 0 and jj == 0:
                                        wait_alone(pe, "pe", s.bank_free, BLK * g + k + 1)
                                    last = mm(k, pos, sl, jj, par, 2 * q + jj, 0, q == 0 and jj == 0, False)
                            last.then_inc(s.pos_used, 1)
                            wait_alone(pe, "pe", s.neg_made, NQ * g + q + 1)
                            for jj in range(2):
                                for k in range(BLK):
                                    last = mm(k, neg, sl, jj, par, 2 * q + jj, 1, False, False)
                            last.then_inc(s.neg_used, 1)
                        q, sl = NQ - 1, SLOT[NQ - 1]
                        wait_alone(pe, "pe", s.neg_made, NQ * g + q + 1)
                        for k in range(BLK):
                            for jj in range(2):
                                mm(k, pos, sl, jj, par, 2 * q + jj, 0, False, False)
                            for jj in range(2):
                                last = mm(k, neg, sl, jj, par, 2 * q + jj, 1, False, jj == 1)
                            last.then_inc(s.bank_ready, 1)
            def transpose_hidden(t, r, u):
                pe.wait_ge(hin_loaded[u], (r + 1) * DMA)
                transpose_rows(hin[:, u, :], s.hT_written)

            def output_tile(t, r, u, more):
                pe.wait_ge(s.hlo_made, t + 1)
                project(2 * u, hT_hi[:, u, :], hT_lo[:, u, :], o_hi, o_lo, 0).then_inc(s.o_written, 1)
                if more:
                    transpose_hidden(t + 1, r + u, 1 - u)
                project(2 * u + 1, hT_hi[:, u, :], hT_lo[:, u, :], o_hi, o_lo, 1).then_inc(s.o_written, 1)

            pe.wait_ge(s.bank_free, BLK * (G + 1))
            transpose_hidden(0, 0, 0)
            pe.wait_ge(s.wo_loaded, DMA)
            with pe.Fori(0, NT // 2 - 1) as r:
                for u in range(2):
                    output_tile(2 * r + u, r, u, True)
            for u in range(2):
                output_tile(NT - 2 + u, NT // 2 - 1, u, u == 0)


_INS = ["x", "adj", "L0_gnn_W_seq", "L0_gnn_a1", "L0_gnn_a2", "L0_gnn_W_out", "L0_gnn_b_out"]


def kernel(**inputs):
    import numpy as _np
    import concourse.bacc as _bacc
    from concourse.bass_utils import run_bass_kernel_spmd as _run

    nc = _bacc.Bacc("TRN2", target_bir_lowering=False, num_devices=1)
    arrays, args = {}, []
    for name in _INS:
        a = _np.ascontiguousarray(inputs[name])
        arrays[f"in_{name}"] = a
        args.append(nc.dram_tensor(f"in_{name}", a.shape, mybir.dt.from_np(a.dtype), kind="ExternalInput").ap())
    out = nc.dram_tensor("out", (N, D), F32, kind="ExternalOutput").ap()
    build(nc, *args, out)
    r = _run(nc, [arrays], core_ids=[0])
    return r.results[0]["out"]
```

```python
import math
from contextlib import ExitStack

import concourse.bass as bass
from concourse import mybir

F32 = mybir.dt.float32
F16 = mybir.dt.float16
BF16 = mybir.dt.bfloat16
F8 = mybir.dt.float8e4
U8 = mybir.dt.uint8
I8 = mybir.dt.int8
U16 = mybir.dt.uint16
ALU = mybir.AluOpType
ACT = mybir.ActivationFunctionType
AX = mybir.AxisListType

P = 128
N, D, H = 4096, 1024, 16
DH = D // H
NT = N // P
KT = D // P
HALF = D // 2
HH = H // 2
BLK = 8
BN = BLK * P
NB = N // BN
G = H * NB
NQ = NT // 2
V1 = DH + 1
V2 = 2 * V1
CT = NT // NB
EPS = 1e-5
W_SCALE = 256.0
H_SCALE = 16.0
V_SCALE = 2.0 ** 15
MASK_ONE = 64.0
AHEAD = 3
CMP_SLOTS = 4
SLOTS = 4
SLOT = [q % SLOTS for q in range(NQ)]
LAST_USE = [max(p - NQ for p in range(NQ + q) if SLOT[p % NQ] == SLOT[q]) for q in range(NQ)]
RS = 9
DMA = 16


def build(nc, x, adj, w_seq, a1, a2, w_out, b_out, out):
    seq_d = nc.dram_tensor("seq_d", (N, D), F32).ap()
    hid_d = nc.dram_tensor("hid_d", (2, N, D), F16).ap()
    wo_d = nc.dram_tensor("wo_d", (2, KT, P, D), F16).ap()
    col_d = nc.dram_tensor("col_d", (P, 2, H, NT), F32).ap()
    s1_d = nc.dram_tensor("s1_d", (H * NT, P), F32).ap()

    x_t = x.rearrange("(t p) c -> t p c", p=P)
    adj_t = adj.rearrange("(t p) c -> t p c", p=P)
    out_t = out.rearrange("(t p) c -> t p c", p=P)
    seq_st = seq_d.rearrange("(t p) c -> t p c", p=P)
    hid_t = hid_d.rearrange("i (t p) c -> i t p c", p=P)
    seq_ld = seq_d.rearrange("(b t p) (h d) -> h b p t d", p=P, t=CT, d=DH)
    hid_st = hid_d.rearrange("i (b t p) (h d) -> i h b p t d", p=P, t=BLK, d=DH)
    s1_g = s1_d.rearrange("(g t) p -> g (t p)", t=BLK)

    ctx = ExitStack()
    with ctx:
        def sb(name, shape, dt, c=None):
            return (c or ctx).enter_context(nc.sbuf_tensor(name, shape, dt))

        def sem(name):
            return ctx.enter_context(nc.semaphore(name))

        ident_f = sb("ident_f", [P, P], F32)
        ph13 = ExitStack()
        adjT = sb("adjT", [P, NT, N], U8, ph13)
        s1 = sb("s1", [P, H, NT], F32, ph13)
        s2 = sb("s2", [P, H, NT], F32, ph13)
        stat = sb("stat", [P, 2, H], F32, ph13)
        stat_r = sb("stat_r", [P, 2, H], F32, ph13)
        ph1 = ExitStack()
        ident_b = sb("ident_b", [P, P], BF16, ph1)
        w_hi = sb("w_hi", [P, KT, D], F16, ph1)
        w_lo = sb("w_lo", [P, KT, D], F16, ph1)
        xin = sb("xin", [P, 2, D], F32, ph1)
        xT_hi = sb("xT_hi", [P, 2, D], F16, ph1)
        xT_lo = sb("xT_lo", [P, 2, D], F16, ph1)
        seq_o = sb("seq_o", [P, D], F32, ph1)
        prod = sb("prod", [P, HALF], F32, ph1)
        adj_in = sb("adj_in", [P, 2, N], BF16, ph1)
        a_row = sb("a_row", [P, 2, DH], F32, ph1)
        smax = sb("smax", [P, H, NT], F32, ph1)
        degree = sb("degree", [P, 2], F32, ph1)
        lonely = sb("lonely", [P, 1], F32, ph1)
        ph1.close()
        ph3 = ExitStack()
        ns2, rowA = s2, s1
        rowC = sb("rowC", [P, H, NT], F32, ph3)
        rhs = sb("rhs", [P, 2, NT, 2, V2], F16, ph3)
        s1row = sb("s1row", [P, 2, BN], F32, ph3)
        cmp = sb("cmp", [P, CMP_SLOTS, 2, BN], U8, ph3)
        pos = sb("pos", [P, SLOTS, 2, BN], U8, ph3)
        neg = sb("neg", [P, SLOTS, 2, BN], U8, ph3)
        stage = sb("stage", [P, CT, DH], F32, ph3)
        vbuf = sb("vbuf", [P, CT, V1], F32, ph3)
        mix = sb("mix", [P, BLK, V2], F32, ph3)
        col = sb("col", [P, 2, CT], F32, ph3)
        vcol = sb("vcol", [P, 2, CT], F32, ph3)
        den = sb("den", [P, 2, BLK], F32, ph3)
        amax = sb("amax", [P, H], F32, ph3)
        ginv = sb("ginv", [P, H], F32, ph3)
        ph3.close()
        tmpa = rhs[:, 0, 0:4 * H * NT // V2 // 2 + 2, :, :].rearrange("p a b c -> p (a b c)")[
            :, 0:4 * H * NT].bitcast(F32).rearrange("p (r h t) -> p r h t", r=2, t=NT)
        colB = rhs[:, 1, 0:4 * H * NT // V2 // 2 + 2, :, :].rearrange("p a b c -> p (a b c)")[
            :, 0:4 * H * NT].bitcast(F32).rearrange("p (r h t) -> p r h t", r=2, t=NT)
        spare = rhs[:, 1, :, :, :].rearrange("p t b c -> p (t b c)").bitcast(F32)
        seq0_at = 2 * H * NT
        prod0_at = seq0_at + NT * DH
        vcol0_at = prod0_at + 2 * CT * V1
        seq0 = spare[:, seq0_at:prod0_at].rearrange("p (t d) -> p t d", d=DH)
        prod0 = spare[:, prod0_at:vcol0_at].rearrange("p (b t c) -> p b t c", b=2, c=V1)
        vcol0 = spare[:, vcol0_at:vcol0_at + 2 * CT].rearrange("p (b t) -> p b t", b=2)
        hid_part = [mix.rearrange("p t c -> p (t c)").bitcast(F16).rearrange("p (t c) -> p t c", t=BLK)[
            :, :, V2 + i * DH:V2 + (i + 1) * DH] for i in range(2)]
        w_raw = adjT[:, NT - KT:NT, :].bitcast(F32)
        wo_raw = adjT[:, 0:4, 3 * N // 4:N].bitcast(F32)
        wo_part = [adjT[:, 4 + 2 * i:6 + 2 * i, 3 * N // 4:N].bitcast(F16) for i in range(2)]
        s1T = cmp[:, 2, :, :].rearrange("p b c -> p (b c)")[:, 0:4 * 4 * P].bitcast(F32)\
            .rearrange("p (k c) -> p k c", k=4)
        ph13.close()
        ph4 = ExitStack()
        o_w = sb("o_w", [P, 2, KT, D], F16, ph4)
        o_hi, o_lo = o_w[:, 0, :, :], o_w[:, 1, :, :]
        hT_hi = sb("hT_hi", [P, 2, D], F16, ph4)
        hT_lo = sb("hT_lo", [P, 2, D], F16, ph4)
        xres = sb("xres", [P, 2, D], F32, ph4)
        b_row = sb("b_row", [P, D], F32, ph4)
        zbuf = sb("zbuf", [P, 2, D], F32, ph4)
        ebuf = sb("ebuf", [P, 2, D], F32, ph4)
        ybuf = sb("ybuf", [P, 2, D], F32, ph4)
        bnst = sb("bnst", [P, 2, 6], F32, ph4)
        mv = sb("mv", [P, 2], F32, ph4)
        nmr = sb("nmr", [P, 2, 2], F32, ph4)
        rstd = sb("rstd", [P, 2], F32, ph4)
        minus_half = sb("minus_half", [P, 1], F32, ph4)
        ph4.close()

        ps = ctx.enter_context(nc.psum_tensor("ps", [P, 8, HALF], F32))
        xT_ps = ps[:, 0:2, :].rearrange("p a c -> p (a c)")
        adjT_ps = [ps[:, 2 + b, :].bitcast(BF16).rearrange("p (g c) -> p g c", c=P) for b in range(2)]
        proj_ps = [ps[:, 4 + b, :] for b in range(4)]

        names = """ident_made a_loaded w_hi_made w_split
            degree_made lonely_made adj_fixed xT_written xhi_made xlo_made adjT_written adjT_act
            adjT_dve proj_written seq_copied seq_reduced prod_made score_made
            stat_made stat_reduced ginv_made expin_made exp_made s1T_written s1T_copied
            s1_stored col_stored s1rep_written first_step first_hi first_made cmp_act cmp_dve
            pos_made neg_made pos_used neg_used rhs_step bank_ready bank_free mixA_made parts_added
            hidden_step den_made den_step hout_made hid_stored stage_loaded
            wo_read wo_step wo_stored wo_loaded b_loaded half_made o_written
            z_made e_in_made e_made y_made y2_made bn_made mv_made rstd_made nmr_made yn_made
            """.split()
        s = type("Sems", (), {n: sem(n) for n in names})
        x_loaded, adj_loaded, seq_stored, s1row_loaded, hT_loaded, \
            xres_loaded, o_stored = ([sem(f"{n}_{u}") for u in range(2)] for n in (
                "x_loaded", "adj_loaded", "seq_stored", "s1row_loaded", "hT_loaded", "xres_loaded", "o_stored"))
        seq0_loaded = [sem(f"seq0_loaded_{c}") for c in range(NB)]
        w_loaded = [sem(f"w_loaded_{k}") for k in range(KT)]

        tally = {e: sem(e + "_tally") for e in ("sp", "pool", "act", "dve", "pe")}

        def wait_alone(eng, name, semaphore, value):
            eng.wait_ge(semaphore, value)
            eng.sem_inc(tally[name], 1)

        def row_loads(g, slot):
            return (g - slot) * (DMA // 2) + DMA

        block = ctx.enter_context(nc.Block())

        @block.sync
        def _(sp):
            sp.dma_start(xin[:, 0, :], x_t[0, :, :]).then_inc(x_loaded[0], DMA)
            for k in range(KT):
                sp.dma_start(w_raw[:, k, :], w_seq[k * P:(k + 1) * P, :]).then_inc(w_loaded[k], DMA)
            sp.dma_start(xin[:, 1, :], x_t[1, :, :]).then_inc(x_loaded[1], DMA)
            sp.dma_start(a_row[:, 0, :], a1.partition_broadcast(P)).then_inc(s.a_loaded, DMA)
            sp.dma_start(a_row[:, 1, :], a2.partition_broadcast(P)).then_inc(s.a_loaded, DMA)

            def load_x(r0, r1):
                with sp.Fori(r0, r1) as r:
                    for u in range(2):
                        sp.wait_ge(s.xT_written, 2 * r + u - 1)
                        sp.dma_start(xin[:, u, :], x_t[2 * r + u, :, :]).then_inc(x_loaded[u], DMA)

            load_x(1, 3 * NT // 8)
            sp.wait_ge(s.wo_stored, 2 * KT * DMA)
            load_x(3 * NT // 8, NT // 2)
            def load_seq0(c):
                for n in range(2):
                    sp.wait_ge(seq_stored[n], ((c + 1) * CT + 1) * DMA)
                sp.dma_start(seq0[:, c * CT:(c + 1) * CT, :], seq_ld[0, c, :, :, :]).then_inc(seq0_loaded[c], DMA)

            sp.wait_ge(s.proj_written, 2 * NT)
            for c in range(NB - 1):
                load_seq0(c)
            sp.wait_ge(s.s1T_copied, 1)
            sp.dma_start(s1_d.rearrange("(k r) c -> r k c", r=P), s1T).then_inc(s.s1_stored, DMA)
            load_seq0(NB - 1)
            sp.wait_ge(s.exp_made, 1)
            sp.dma_start(col_d, colB).then_inc(s.col_stored, DMA)

            def load_row(g, slot):
                sp.dma_start(s1row[:, slot, :], s1_g[g, :].partition_broadcast(P)).then_inc(s1row_loaded[slot], DMA)

            def load_stage(head, part):
                sp.dma_start(stage[:, :, :], seq_ld[head, part, :, :, :]).then_inc(s.stage_loaded, DMA)
                sp.dma_start(col[:, :, :], col_d[:, :, head, bass.ds(part * CT, CT)]).then_inc(s.stage_loaded, DMA)

            sp.wait_ge(s.s1_stored, DMA)
            load_row(1, 1)
            sp.wait_ge(s.s1T_written, 1)
            sp.wait_ge(s.col_stored, DMA)
            load_stage(1, 0)

            def store_hidden(head, part, g):
                sp.wait_ge(s.hout_made, g + 1)
                for i in range(2):
                    sp.dma_start(hid_st[i, head, part, :, :, :], hid_part[i]).then_inc(s.hid_stored, DMA)

            def next_row(g, slot):
                wait_alone(sp, "sp", s.cmp_act, (g + 1) * (NT * 3 // 4))
                wait_alone(sp, "sp", s.cmp_dve, (g + 1) * (NT // 4))
                load_row(g + 2, slot)

            with sp.Fori(0, H - 2) as hd:
                for b in range(NB):
                    g, c = hd * NB + b, b + 5
                    store_hidden(hd, b, g)
                    next_row(g, b % 2)
                    sp.wait_ge(s.rhs_step, RS * (g + 5))
                    load_stage(hd + c // NB, c % NB)
            for g in range(G - 2 * NB, G - 1):
                store_hidden(g // NB, g % NB, g)
                if g + 2 < G:
                    next_row(g, g % 2)
                if g + 5 < G:
                    sp.wait_ge(s.rhs_step, RS * (g + 5))
                    load_stage((g + 5) // NB, (g + 5) % NB)
            sp.wait_ge(s.neg_made, NQ * (G - 1) + KT // 2)
            sp.dma_start(o_w[:, :, :, :], wo_d.rearrange("i k p c -> p i k c")).then_inc(s.wo_loaded, DMA)
            sp.wait_ge(s.neg_made, NQ * (G - 1) + KT)
            sp.dma_start(b_row[:, :], b_out.partition_broadcast(P)).then_inc(s.b_loaded, DMA)

            def load_out(t, u):
                for i, dst in enumerate((hT_hi, hT_lo)):
                    sp.dma_start_transpose(dst[:, u, :].rearrange("p (k c) -> p k c", c=P),
                                           hid_t[i, t, :, :]).then_inc(hT_loaded[u], DMA)
                sp.dma_start(xres[:, u, :], x_t[t, :, :]).then_inc(xres_loaded[u], DMA)

            sp.wait_ge(s.hid_stored, 2 * (G - NB + 1) * DMA)
            load_out(0, 0)
            load_out(1, 1)
            store_hidden(H - 1, NB - 1, G - 1)
            sp.wait_ge(s.hid_stored, 2 * G * DMA)
            with sp.Fori(1, NT // 2) as r:
                for u in range(2):
                    wait_alone(sp, "sp", s.o_written, 2 * (2 * r + u - 1))
                    wait_alone(sp, "sp", s.y_made, 2 * (2 * r + u - 1))
                    load_out(2 * r + u, u)
            for u in range(2):
                sp.wait_ge(o_stored[u], (NT // 2 + 1) * DMA)

        @block.gpsimd
        def _(pool):
            pool.dma_start(adj_in[:, 0, :], adj_t[0, :, :]).then_inc(adj_loaded[0], DMA)
            for i, m in enumerate((ident_b, ident_f)):
                nc.gpsimd.memset(m[:, :], 0.0).then_inc(s.ident_made, 1)
                pool.wait_ge(s.ident_made, 2 * i + 1)
                nc.gpsimd.affine_select(out=m[:, :], in_=m[:, :], compare_op=ALU.not_equal, fill=1.0,
                                        base=0, pattern=[[-1, P]], channel_multiplier=1)\
                    .then_inc(s.ident_made, 1)
            def load_adj(r0, r1):
                with pool.Fori(r0, r1) as r:
                    for u in range(2):
                        pool.wait_ge(s.adjT_written, 4 * (2 * r + u - 1))
                        pool.dma_start(adj_in[:, u, :], adj_t[2 * r + u, :, :]).then_inc(adj_loaded[u], DMA)

            pool.wait_ge(w_loaded[0], DMA)
            pool.dma_start(adj_in[:, 1, :], adj_t[1, :, :]).then_inc(adj_loaded[1], DMA)
            for k in range(KT):
                pool.dma_start(wo_raw, w_out[k * P:(k + 1) * P, :].rearrange("p (a c) -> p a c", a=4))\
                    .then_inc(s.wo_read, DMA)
                load_adj(k + 1, k + 2)
                pool.wait_ge(s.wo_read, (k + 1) * DMA)
                nc.gpsimd.tensor_scalar(wo_raw, wo_raw, W_SCALE, None, ALU.mult).then_inc(s.wo_step, 1)
                pool.wait_ge(s.wo_step, 3 * k + 1)
                if k:
                    pool.wait_ge(s.wo_stored, 2 * k * DMA)
                hi, lo = (w.rearrange("p i (a c) -> p i a c", a=2) for w in wo_part)
                whole = wo_raw.rearrange("p (i a) c -> p i a c", a=2)
                nc.gpsimd.tensor_copy(hi, whole).then_inc(s.wo_step, 1)
                pool.wait_ge(s.wo_step, 3 * k + 2)
                nc.gpsimd.tensor_tensor(lo, whole, hi, ALU.subtract).then_inc(s.wo_step, 1)
                pool.wait_ge(s.wo_step, 3 * k + 3)
                for i, part in enumerate(wo_part):
                    pool.dma_start(wo_d[i, k, :, :].rearrange("p (a c) -> p a c", a=2), part)\
                        .then_inc(s.wo_stored, DMA)
            load_adj(KT + 1, NT // 2)
            pool.wait_ge(s.stat_made, 2)
            nc.gpsimd.partition_all_reduce(stat_r[:, :, :], stat[:, :, :], P, bass.bass_isa.ReduceOp.max)\
                .then_inc(s.stat_reduced, 1)
            nc.gpsimd.sem_inc(s.rhs_step, RS)
            pool.wait_ge(s.exp_made, 1)
            pool.wait_ge(s.ginv_made, 1)

            def chunk(c, head, part, par):
                if isinstance(c, int) and c < NB:
                    pool.wait_ge(seq0_loaded[c], DMA)
                    rows, cols = seq0[:, c * CT:(c + 1) * CT, :], colB[:, :, 0, c * CT:(c + 1) * CT]
                else:
                    pool.wait_ge(s.stage_loaded, (c - NB + 1) * 2 * DMA)
                    rows, cols = stage[:, :, :], col[:, :, :]
                if not isinstance(c, int):
                    wait_alone(pool, "pool", s.bank_ready, BLK * NB * (head - 1))
                ts = bass.ds(part * CT, CT)
                nc.gpsimd.tensor_tensor(vcol[:, :, :], cols,
                                        ginv[:, bass.ds(head, 1)].unsqueeze(2).to_broadcast([P, 2, CT]),
                                        ALU.mult).then_inc(s.rhs_step, 1)
                pool.wait_ge(s.rhs_step, RS * c + 1)
                for br in range(2):
                    n = RS * c + 1 + 4 * br
                    nc.gpsimd.tensor_tensor(vbuf[:, :, 0:DH], rows,
                                            vcol[:, br, :].unsqueeze(2).to_broadcast([P, CT, DH]),
                                            ALU.mult).then_inc(s.rhs_step, 1)
                    nc.gpsimd.tensor_copy(vbuf[:, :, DH], cols[:, br, :]).then_inc(s.rhs_step, 1)
                    pool.wait_ge(s.rhs_step, n + 2)
                    nc.gpsimd.tensor_copy(rhs[:, par, ts, br, 0:V1], vbuf[:, :, :]).then_inc(s.rhs_step, 1)
                    wait_alone(pool, "pool", s.rhs_step, n + 3)
                    nc.gpsimd.tensor_tensor(rhs[:, par, ts, br, V1:V2], vbuf[:, :, :],
                                            rhs[:, par, ts, br, 0:V1], ALU.subtract)\
                        .then_inc(s.rhs_step, 1)
                    pool.wait_ge(s.rhs_step, n + 4)

            for c in range(1, NB):
                chunk(c, 0, c, 0)

            def combine(g):
                pool.wait_ge(s.bank_free, BLK * (g + 2))
                both = mix[:, :, 0:DH]
                nc.gpsimd.tensor_tensor(both, both, mix[:, :, V1:V1 + DH], ALU.add)\
                    .then_inc(s.parts_added, 1)
                pool.wait_ge(s.parts_added, g + 1)
                wait_alone(pool, "pool", s.den_made, g + 1)
                nc.gpsimd.tensor_tensor(both, both,
                                        den[:, 1, :].unsqueeze(2).to_broadcast([P, BLK, DH]), ALU.mult)\
                    .then_inc(s.hidden_step, 1)
                wait_alone(pool, "pool", s.hidden_step, 2 * g + 1)
                nc.gpsimd.tensor_copy(hid_part[0], both).then_inc(s.hidden_step, 1)
                wait_alone(pool, "pool", s.hidden_step, 2 * g + 2)
                nc.gpsimd.tensor_tensor(hid_part[1], both, hid_part[0], ALU.subtract)\
                    .then_inc(s.hout_made, 1)

            pool.wait_ge(s.first_made, 2)
            for b in range(NB):
                chunk(b + NB, 1, b, 1)
                combine(b)
            with pool.Fori(1, H - 1) as hd:
                par = (hd + 1) % 2
                for b in range(NB):
                    chunk((hd + 1) * NB + b, hd + 1, b, par)
                    combine(hd * NB + b)
            for b in range(NB):
                combine((H - 1) * NB + b)
            pool.wait_ge(s.hid_stored, 2 * G * DMA)
            nc.gpsimd.memset(minus_half[:, :], -0.5).then_inc(s.half_made, 1)
            pool.wait_ge(s.half_made, 1)
            with pool.Fori(0, NT // 2) as r:
                for u in range(2):
                    t = 2 * r + u
                    pool.wait_ge(s.mv_made, 2 * t + 2)
                    nc.gpsimd.tensor_tensor(rstd[:, u:u + 1], mv[:, 1:2], minus_half[:, :], ALU.pow)\
                        .then_inc(s.rstd_made, 1)

        @block.scalar
        def _(act):
            def degrees(t, r, u):
                act.wait_ge(adj_loaded[u], (r + 1) * DMA)
                nc.scalar.activation(adj_in[:, u, :], adj_in[:, u, :], ACT.Copy,
                                     accum_out=degree[:, u:u + 1]).then_inc(s.degree_made, 1)

            def x_high(t, u):
                act.wait_ge(s.xT_written, t + 1)
                nc.scalar.activation(xT_hi[:, u, :], xT_ps, ACT.Copy).then_inc(s.xhi_made, 1)

            def adj_copy(t, g):
                act.wait_ge(s.adjT_written, 4 * t + g + 1)
                nc.scalar.activation(adjT[:, 8 * g:8 * g + 8, bass.ds(t * P, P)], adjT_ps[g % 2],
                                     ACT.Copy).then_inc(s.adjT_act, 1)

            def seq_copy(t, u, n):
                act.wait_ge(s.proj_written, 2 * t + n + 1)
                act.wait_ge(s.seq_reduced, 2 * t + n + 1)
                act.wait_ge(seq_stored[n], (t + 1) * DMA)
                nc.scalar.activation(seq_o[:, n * HALF:(n + 1) * HALF], proj_ps[2 * u + n],
                                     ACT.Copy, scale=1.0 / W_SCALE).then_inc(s.seq_copied, 1)
                act.wait_ge(s.seq_copied, 2 * t + n + 1)
                act.dma_start(seq_st[t, :, n * HALF:(n + 1) * HALF],
                              seq_o[:, n * HALF:(n + 1) * HALF]).then_inc(seq_stored[n], DMA)

            def project_tile(t, r, u, more, first=False):
                adj_copy(t, 0)
                if more and not first:
                    degrees(t + 1, r + u, 1 - u)
                seq_copy(t, u, 0)
                adj_copy(t, 2)
                if more:
                    x_high(t + 1, 1 - u)
                adj_copy(t, 3)
                if first:
                    degrees(t + 1, r + u, 1 - u)
                seq_copy(t, u, 1)

            x_high(0, 0)
            for k in range(KT):
                if k == 1:
                    degrees(0, 0, 0)
                act.wait_ge(w_loaded[k], DMA)
                nc.scalar.activation(w_hi[:, k, :], w_raw[:, k, :], ACT.Copy, scale=W_SCALE)\
                    .then_inc(s.w_hi_made, 1)
            for u in range(2):
                project_tile(u, 0, u, True, first=(u == 0))
            with act.Fori(1, NT // 2 - 1) as r:
                for u in range(2):
                    project_tile(2 * r + u, r, u, True)
            for u in range(2):
                project_tile(NT - 2 + u, NT // 2 - 1, u, u == 0)
            act.wait_ge(s.s1T_written, 1)
            for n in range(2):
                act.wait_ge(seq_stored[n], (NT + 1) * DMA)
            nc.scalar.activation(s1T, ps[:, 0, :].rearrange("p (k c) -> p k c", k=4), ACT.Copy)\
                .then_inc(s.s1T_copied, 1)
            act.wait_ge(s.s1rep_written, 1)
            nc.scalar.activation(s1row[:, 0, :].rearrange("p (a c) -> p a c", a=2), ps[:, 1:3, :], ACT.Copy)\
                .then_inc(s1row_loaded[0], DMA)
            act.wait_ge(s.expin_made, 2)
            nc.scalar.activation(colB[:, :, :, :], colB[:, :, :, :], ACT.Exp).then_inc(s.exp_made, 1)

            def compare(slot_row, head, j, slot, jj):
                nc.scalar.activation(cmp[:, slot, jj, :].bitcast(I8), s1row[:, slot_row, :], ACT.Sign,
                                     scale=-1.0, bias=ns2[:, head, j:j + 1]).then_inc(s.cmp_act, 1)

            def pairs(g, head, slot_row, qs):
                for q in qs:
                    if q == 0:
                        act.wait_ge(s1row_loaded[slot_row], row_loads(g, slot_row))
                    if not (isinstance(g, int) and g == 0 and q < CMP_SLOTS):
                        wait_alone(act, "act", s.pos_made, NQ * g + q - CMP_SLOTS + 1)
                    compare(slot_row, head, 2 * q, q % CMP_SLOTS, 0)
                    if q % 2 == 0:
                        compare(slot_row, head, 2 * q + 1, q % CMP_SLOTS, 1)

            def evacuate(g, head, part):
                if not isinstance(g, int) or g > 0:
                    act.wait_ge(s.hid_stored, 2 * g * DMA)
                for k in range(BLK):
                    act.wait_ge(s.bank_ready, BLK * g + k + 1)
                    nc.scalar.activation(mix[:, k, :], ps[:, k, 0:V2], ACT.Copy,
                                         scale=rowA[:, head, bass.ds(part * BLK + k, 1)])\
                        .then_inc(s.mixA_made, 1)

            act.wait_ge(s.ginv_made, 2)
            pairs(0, 0, 0, [0])
            for br in range(2):
                act.wait_ge(s.first_step, 3 + br)
                nc.scalar.activation(rhs[:, 0, 0:CT, br, 0:V1], prod0[:, br, :, :], ACT.Copy)\
                    .then_inc(s.first_hi, 1)
            early, late = range(CMP_SLOTS), range(CMP_SLOTS, NQ)
            pairs(0, 0, 0, [1])
            act.wait_ge(s.s1_stored, DMA)
            pairs(0, 0, 0, [2, 3])
            act.wait_ge(s.expin_made, 4)
            nc.scalar.activation(rowA[:, :, :], rowA[:, :, :], ACT.Exp).then_inc(s.exp_made, 1)
            nc.scalar.activation(rowC[:, :, :], rowC[:, :, :], ACT.Exp).then_inc(s.exp_made, 1)
            pairs(0, 0, 0, late)
            pairs(1, 0, 1, early)
            act.wait_ge(s.exp_made, 3)
            evacuate(0, 0, 0)
            with act.Fori(0, H - 1) as hd:
                for b in range(1, NB + 1):
                    g, n = hd * NB + b, b + 1
                    head, part = hd + b // NB, b % NB
                    pairs(g, head, b % 2, late)
                    pairs(g + 1, hd + n // NB, n % 2, early)
                    evacuate(g, head, part)
            for g in range(G - NB + 1, G):
                pairs(g, H - 1, g % 2, late)
                if g + 1 < G:
                    pairs(g + 1, H - 1, (g + 1) % 2, early)
                evacuate(g, H - 1, g % NB)
            def output_tile(t, u):
                for n in range(2):
                    cs = slice(n * HALF, (n + 1) * HALF)
                    act.wait_ge(s.e_in_made, 2 * t + n + 1)
                    nc.scalar.activation(ebuf[:, u, cs], ebuf[:, u, cs], ACT.Exp).then_inc(s.e_made, 1)
                act.wait_ge(s.nmr_made, t + 1)
                nc.scalar.activation(ybuf[:, u, :], ybuf[:, u, :], ACT.Identity,
                                     scale=rstd[:, u:u + 1], bias=nmr[:, u, 0:1]).then_inc(s.yn_made, 1)
                act.wait_ge(s.yn_made, t + 1)
                act.dma_start(out_t[t, :, :], ybuf[:, u, :]).then_inc(o_stored[u], DMA)

            with act.Fori(0, NT // 2) as r:
                for u in range(2):
                    output_tile(2 * r + u, u)

        @block.vector
        def _(dve):
            nc.vector.sem_inc(s.seq_reduced, 2)
            for n in range(2):
                nc.vector.sem_inc(seq_stored[n], DMA)
            def fix_adj(t, u):
                dve.wait_ge(s.degree_made, t + 1)
                nc.vector.tensor_scalar(lonely[:, :], degree[:, u:u + 1], 0.0, None, ALU.is_equal)\
                    .then_inc(s.lonely_made, 1)
                dve.wait_ge(s.lonely_made, t + 1)
                nc.vector.tensor_scalar(adj_in[:, u, :], adj_in[:, u, :], lonely[:, 0:1], MASK_ONE,
                                        ALU.max, ALU.mult).then_inc(s.adj_fixed, 1)

            def x_low(t, u):
                dve.wait_ge(s.xhi_made, t + 1)
                nc.vector.tensor_tensor(xT_lo[:, u, :], xT_ps, xT_hi[:, u, :], ALU.subtract)\
                    .then_inc(s.xlo_made, 1)

            def adj_copy(t):
                dve.wait_ge(s.adjT_written, 4 * t + 2)
                nc.vector.tensor_copy(adjT[:, 8:16, bass.ds(t * P, P)], adjT_ps[1])\
                    .then_inc(s.adjT_dve, 1)

            def scores(t, n):
                dve.wait_ge(s.seq_copied, 2 * t + n + 1)
                half = seq_o[:, n * HALF:(n + 1) * HALF].rearrange("p (h d) -> p h d", d=DH)
                pr = prod[:, :].rearrange("p (h d) -> p h d", d=DH)
                hs = slice(n * HH, (n + 1) * HH)
                for v, dst in ((0, s1), (1, s2)):
                    i = 4 * t + 2 * n + v
                    nc.vector.tensor_tensor(pr, half, a_row[:, v, :].unsqueeze(1)
                                            .to_broadcast([P, HH, DH]), ALU.mult).then_inc(s.prod_made, 1)
                    dve.wait_ge(s.prod_made, i + 1)
                    nc.vector.tensor_reduce(dst[:, hs, bass.ds(t, 1)].rearrange("p h o -> p (h o)"),
                                            pr, AX.X, ALU.add).then_inc(s.score_made, 1)
                    dve.wait_ge(s.score_made, i + 1)
                nc.vector.tensor_reduce(smax[:, hs, bass.ds(t, 1)].rearrange("p h o -> p (h o)"),
                                        half, AX.X, ALU.max, apply_absolute_value=True)\
                    .then_inc(s.seq_reduced, 1)

            def project_tile(t, u, more, first=False):
                adj_copy(t)
                if more and not first:
                    fix_adj(t + 1, 1 - u)
                scores(t, 0)
                if more:
                    x_low(t + 1, 1 - u)
                if first:
                    fix_adj(t + 1, 1 - u)
                scores(t, 1)

            x_low(0, 0)
            for k in range(KT):
                if k == 1:
                    fix_adj(0, 0)
                dve.wait_ge(s.w_hi_made, k + 1)
                nc.vector.scalar_tensor_tensor(out=w_lo[:, k, :], in0=w_raw[:, k, :], scalar=W_SCALE,
                                               in1=w_hi[:, k, :], op0=ALU.mult, op1=ALU.subtract)\
                    .then_inc(s.w_split, 1)
            dve.wait_ge(s.a_loaded, 2 * DMA)
            for u in range(2):
                project_tile(u, u, True, first=(u == 0))
            with dve.Fori(1, NT // 2 - 1) as r:
                for u in range(2):
                    project_tile(2 * r + u, u, True)
            for u in range(2):
                project_tile(NT - 2 + u, u, u == 0)
            dve.wait_ge(s.seq_reduced, 2 * NT + 2)
            dve.wait_ge(s.score_made, 4 * NT)
            nc.vector.tensor_reduce(stat[:, 0, :], s2[:, :, :], AX.X, ALU.max).then_inc(s.stat_made, 1)
            nc.vector.tensor_reduce(stat[:, 1, :], smax[:, :, :], AX.X, ALU.max).then_inc(s.stat_made, 1)
            dve.wait_ge(s.stat_reduced, 1)
            dve.wait_ge(s.s1T_written, 1)
            top = stat_r[:, 0, :].unsqueeze(2).to_broadcast([P, H, NT])
            nc.vector.tensor_tensor(tmpa[:, 1, :, :], s2[:, :, :], top, ALU.subtract).then_inc(s.den_step, 1)
            nc.vector.tensor_scalar(amax[:, :], stat_r[:, 1, :], 1e-30, None, ALU.max).then_inc(s.den_step, 1)
            dve.wait_ge(s.den_step, 1)
            nc.vector.tensor_scalar(colB[:, 0, :, :], tmpa[:, 1, :, :], math.log(V_SCALE), None, ALU.add)\
                .then_inc(s.expin_made, 1)
            nc.vector.tensor_scalar(colB[:, 1, :, :], tmpa[:, 1, :, :], 0.2, math.log(V_SCALE),
                                    ALU.mult, ALU.add).then_inc(s.expin_made, 1)
            dve.wait_ge(s.den_step, 2)
            nc.vector.reciprocal(ginv[:, :], amax[:, :]).then_inc(s.ginv_made, 1)
            nc.vector.tensor_tensor(tmpa[:, 0, :, :], s1[:, :, :], top, ALU.add).then_inc(s.den_step, 1)
            nc.vector.tensor_scalar(ns2[:, :, :], s2[:, :, :], -1.0, None, ALU.mult).then_inc(s.ginv_made, 1)
            dve.wait_ge(s.den_step, 3)
            dve.wait_ge(s.s1rep_written, 1)
            nc.vector.tensor_scalar(rowA[:, :, :], tmpa[:, 0, :, :], 0.8, 0.0, ALU.mult, ALU.min)\
                .then_inc(s.expin_made, 1)
            nc.vector.tensor_scalar(rowC[:, :, :], tmpa[:, 0, :, :], -0.8, 0.0, ALU.mult, ALU.min)\
                .then_inc(s.expin_made, 1)
            dve.wait_ge(s.exp_made, 1)
            dve.wait_ge(s.ginv_made, 1)
            nc.vector.tensor_tensor(vcol0, colB[:, :, 0, 0:CT], ginv[:, 0:1].unsqueeze(2).to_broadcast([P, 2, CT]),
                                    ALU.mult).then_inc(s.first_step, 1)
            nc.vector.tensor_copy(prod0[:, :, :, DH], colB[:, :, 0, 0:CT]).then_inc(s.first_step, 1)
            dve.wait_ge(s.first_step, 2)
            dve.wait_ge(seq0_loaded[0], DMA)
            for br in range(2):
                nc.vector.tensor_tensor(prod0[:, br, :, 0:DH], seq0[:, 0:CT, :],
                                        vcol0[:, br, :].unsqueeze(2).to_broadcast([P, CT, DH]),
                                        ALU.mult).then_inc(s.first_step, 1)
            dve.wait_ge(s.s1T_copied, 1)
            dve.wait_ge(s1row_loaded[0], DMA)
            nc.vector.sem_inc(s.bank_free, BLK)
            for n in range(2):
                dve.wait_ge(seq_stored[n], (NT + 1) * DMA)

            def compare(pair):
                g, head, part, row, q = pair
                if q == 1:
                    dve.wait_ge(s1row_loaded[row], row_loads(g, row))
                if not (isinstance(g, int) and g == 0 and q < CMP_SLOTS):
                    dve.wait_ge(s.pos_made, NQ * g + q - CMP_SLOTS + 1)
                nc.vector.tensor_scalar(cmp[:, q % CMP_SLOTS, 1, :], s1row[:, row, :],
                                        ns2[:, head, 2 * q + 1:2 * q + 2], MASK_ONE,
                                        ALU.is_gt, ALU.mult).then_inc(s.cmp_dve, 1)

            def adj_pair(part, q):
                return adjT[:, 2 * q:2 * q + 2, bass.ds(part * BN, BN)].bitcast(U16)

            def make_pos(pair):
                g, head, part, row, q = pair
                if q % 2 == 1:
                    dve.wait_ge(s.cmp_dve, NQ // 2 * g + q // 2 + 1)
                dve.wait_ge(s.cmp_act, 3 * NQ // 2 * g + 3 * (q // 2) + 2 + q % 2)
                last = LAST_USE[q]
                start = isinstance(g, int) and g == 0
                if not (start and last < 0):
                    dve.wait_ge(s.neg_made, NQ * g + last + 1)
                if last == -1:
                    if not start:
                        dve.wait_ge(s.bank_ready, BLK * g)
                elif not (start and last < 0):
                    dve.wait_ge(s.pos_used, (NQ - 1) * g + last + 1 + (last < 0))
                nc.vector.tensor_tensor(pos[:, SLOT[q], :, :].bitcast(U16), adj_pair(part, q),
                                        cmp[:, q % CMP_SLOTS, :, :].bitcast(U16),
                                        ALU.bitwise_and).then_inc(s.pos_made, 1)

            def make_neg(pair):
                g, head, part, row, q = pair
                last = LAST_USE[q]
                if last != -1 and not (isinstance(g, int) and g == 0 and last < 0):
                    dve.wait_ge(s.neg_used, (NQ - 1) * g + last + 1 + (last < 0))
                dve.wait_ge(s.pos_made, NQ * g + q + 1)
                nc.vector.tensor_tensor(neg[:, SLOT[q], :, :].bitcast(U16), adj_pair(part, q),
                                        pos[:, SLOT[q], :, :].bitcast(U16),
                                        ALU.bitwise_xor).then_inc(s.neg_made, 1)

            def masks(pairs):
                if pairs[0][-1] % 2 == 1:
                    compare(pairs[0])
                for i, pair in enumerate(pairs):
                    make_pos(pair)
                    if i + 1 < len(pairs) and pairs[i + 1][-1] % 2 == 1:
                        compare(pairs[i + 1])
                    if i > 0:
                        make_neg(pairs[i - 1])
                make_neg(pairs[-1])

            def evacuate(g, head, part):
                for k in range(BLK):
                    dve.wait_ge(s.mixA_made, BLK * g + k + 1)
                    nc.vector.scalar_tensor_tensor(out=mix[:, k, :], in0=ps[:, k, V2:2 * V2],
                                                   scalar=rowC[:, head, bass.ds(part * BLK + k, 1)],
                                                   in1=mix[:, k, :], op0=ALU.mult, op1=ALU.add)\
                        .then_inc(s.bank_free, 1)
                dve.wait_ge(s.bank_free, BLK * (g + 2))
                if not (isinstance(g, int) and g == 0):
                    dve.wait_ge(s.hout_made, g)
                nc.vector.tensor_tensor(den[:, 0, :], mix[:, :, DH], mix[:, :, V1 + DH], ALU.add)\
                    .then_inc(s.den_step, 1)
                dve.wait_ge(s.den_step, 2 * g + 4)
                nc.vector.reciprocal(den[:, 1, :], den[:, 0, :]).then_inc(s.den_step, 1)
                dve.wait_ge(s.den_step, 2 * g + 5)
                nc.vector.tensor_scalar(den[:, 1, :], den[:, 1, :], amax[:, bass.ds(head, 1)], H_SCALE,
                                        ALU.mult, ALU.mult)\
                    .then_inc(s.den_made, 1)

            masks([(0, 0, 0, 0, 0)])
            for br in range(2):
                dve.wait_ge(s.first_hi, br + 1)
                nc.vector.tensor_tensor(rhs[:, 0, 0:CT, br, V1:V2], prod0[:, br, :, :],
                                        rhs[:, 0, 0:CT, br, 0:V1], ALU.subtract).then_inc(s.first_made, 1)
            masks([(0, 0, 0, 0, q) for q in range(1, NQ)] + [(1, 0, 1, 1, q) for q in range(AHEAD)])
            dve.wait_ge(s.exp_made, 3)
            evacuate(0, 0, 0)
            with dve.Fori(0, H - 1) as hd:
                for b in range(1, NB + 1):
                    g, n = hd * NB + b, b + 1
                    head, part = hd + b // NB, b % NB
                    masks([(g, head, part, b % 2, q) for q in range(AHEAD, NQ)]
                          + [(g + 1, hd + n // NB, n % NB, n % 2, q) for q in range(AHEAD)])
                    evacuate(g, head, part)
            for g in range(G - NB + 1, G):
                masks([(g, H - 1, g % NB, g % 2, q) for q in range(AHEAD, NQ)]
                      + [(g + 1, H - 1, (g + 1) % NB, (g + 1) % 2, q) for q in range(AHEAD) if g + 1 < G])
                evacuate(g, H - 1, g % NB)
            dve.wait_ge(s.b_loaded, DMA)
            for u in range(2):
                nc.vector.sem_inc(o_stored[u], DMA)

            def output_tile(t, r, u):
                for n in range(2):
                    cs = slice(n * HALF, (n + 1) * HALF)
                    dve.wait_ge(s.o_written, 2 * t + n + 1)
                    nc.vector.scalar_tensor_tensor(out=zbuf[:, u, cs], in0=proj_ps[2 * u + n],
                                                   scalar=1.0 / (W_SCALE * H_SCALE), in1=b_row[:, cs],
                                                   op0=ALU.mult, op1=ALU.add).then_inc(s.z_made, 1)
                    dve.wait_ge(s.z_made, 2 * t + n + 1)
                    nc.vector.tensor_scalar(ebuf[:, u, cs], zbuf[:, u, cs], 0.0, None, ALU.min)\
                        .then_inc(s.e_in_made, 1)
                    dve.wait_ge(s.e_in_made, 2 * t + n + 1)
                    if n == 0:
                        dve.wait_ge(xres_loaded[u], (r + 1) * DMA)
                    nc.vector.scalar_tensor_tensor(out=zbuf[:, u, cs], in0=zbuf[:, u, cs], scalar=0.0,
                                                   in1=xres[:, u, cs], op0=ALU.max, op1=ALU.add)\
                        .then_inc(s.y_made, 1)
                    dve.wait_ge(s.y_made, 2 * t + n + 1)
                    dve.wait_ge(s.e_made, 2 * t + n + 1)
                    if n == 0:
                        dve.wait_ge(o_stored[u], (r + 1) * DMA)
                    nc.vector.scalar_tensor_tensor(out=ybuf[:, u, cs], in0=ebuf[:, u, cs], scalar=-1.0,
                                                   in1=zbuf[:, u, cs], op0=ALU.add, op1=ALU.add)\
                        .then_inc(s.y2_made, 1)
                    dve.wait_ge(s.y2_made, 2 * t + n + 1)
                    nc.vector.bn_stats(bnst[:, n, :], ybuf[:, u, cs]).then_inc(s.bn_made, 1)
                wait_alone(dve, "dve", s.bn_made, 2 * t + 2)
                nc.vector.bn_aggr(mv[:, :], bnst[:, :, :]).then_inc(s.mv_made, 1)
                dve.wait_ge(s.mv_made, 2 * t + 1)
                nc.vector.tensor_scalar(mv[:, 1:2], mv[:, 1:2], EPS, None, ALU.add).then_inc(s.mv_made, 1)
                dve.wait_ge(s.rstd_made, t + 1)
                nc.vector.scalar_tensor_tensor(out=nmr[:, u, 0:1], in0=mv[:, 0:1], scalar=-1.0,
                                               in1=rstd[:, u:u + 1], op0=ALU.mult, op1=ALU.mult)\
                    .then_inc(s.nmr_made, 1)

            with dve.Fori(0, NT // 2) as r:
                for u in range(2):
                    output_tile(2 * r + u, r, u)

        @block.tensor
        def _(pe):
            pe.wait_ge(s.ident_made, 4)

            def transpose_rows(src, done):
                for k in range(KT):
                    last = nc.tensor.transpose(xT_ps[:, k * P:(k + 1) * P], src[:, k * P:(k + 1) * P],
                                               ident_f[:, :])
                last.then_inc(done, 1)

            def project(bank, lhs_hi, lhs_lo, r_hi, r_lo, n, arriving=False):
                cs = slice(n * HALF, (n + 1) * HALF)
                for k in range(KT):
                    hi, lo = lhs_hi[:, k * P:(k + 1) * P], lhs_lo[:, k * P:(k + 1) * P]
                    if arriving:
                        pe.wait_ge(s.w_split, k + 1)
                    nc.tensor.matmul(proj_ps[bank], hi, r_hi[:, k, cs], start=(k == 0), stop=False)
                    nc.tensor.matmul(proj_ps[bank], hi, r_lo[:, k, cs], start=False, stop=False)
                    last = nc.tensor.matmul(proj_ps[bank], lo, r_hi[:, k, cs], start=False,
                                            stop=(k == KT - 1))
                return last

            def transpose_x(t, r, u):
                pe.wait_ge(x_loaded[u], (r + 1) * DMA)
                transpose_rows(xin[:, u, :], s.xT_written)

            def transpose_adj(t, u, g):
                for i in range(8):
                    j = 8 * g + i
                    last = nc.tensor.transpose(adjT_ps[g % 2][:, i, :],
                                               adj_in[:, u, j * P:(j + 1) * P], ident_b[:, :])
                last.then_inc(s.adjT_written, 1)

            def project_tile(t, r, u, more, arriving=False):
                pe.wait_ge(s.adj_fixed, t + 1)
                if not isinstance(t, int) or t > 0:
                    pe.wait_ge(s.adjT_act, 3 * t - 1)
                transpose_adj(t, u, 0)
                if not isinstance(t, int) or t > 0:
                    pe.wait_ge(s.adjT_act, 3 * t)
                transpose_adj(t, u, 1)
                pe.wait_ge(s.xlo_made, t + 1)
                project(2 * u, xT_hi[:, u, :], xT_lo[:, u, :], w_hi, w_lo, 0, arriving)\
                    .then_inc(s.proj_written, 1)
                pe.wait_ge(s.adjT_act, 3 * t + 1)
                transpose_adj(t, u, 2)
                pe.wait_ge(s.adjT_dve, t + 1)
                transpose_adj(t, u, 3)
                if more:
                    transpose_x(t + 1, r + u, 1 - u)
                project(2 * u + 1, xT_hi[:, u, :], xT_lo[:, u, :], w_hi, w_lo, 1).then_inc(s.proj_written, 1)

            transpose_x(0, 0, 0)
            for u in range(2):
                project_tile(u, 0, u, True, arriving=(u == 0))
            with pe.Fori(1, NT // 2 - 1) as r:
                for u in range(2):
                    project_tile(2 * r + u, r, u, True)
            for u in range(2):
                project_tile(NT - 2 + u, NT // 2 - 1, u, u == 0)
            pe.wait_ge(s.seq_reduced, 2 * NT + 2)
            for k in range(4):
                last = nc.tensor.transpose(ps[:, 0, k * P:(k + 1) * P],
                                           s1[:, 4 * k:4 * k + 4, :].rearrange("p h t -> p (h t)"),
                                           ident_f[:, :])
            last.then_inc(s.s1T_written, 1)
            pe.wait_ge(s.xlo_made, NT)
            pe.wait_ge(s.adjT_act, 3 * NT)
            for k in range(BLK):
                last = nc.tensor.transpose(ps[:, 1 + k // 4, k % 4 * P:(k % 4 + 1) * P],
                                           s1[:, 0, k:k + 1].to_broadcast([P, P]), ident_f[:, :])
            last.then_inc(s.s1rep_written, 1)
            pe.wait_ge(s.s1T_copied, 1)
            pe.wait_ge(s1row_loaded[0], DMA)
            pe.wait_ge(s.adjT_dve, NT)
            pe.wait_ge(s.seq_copied, 2 * NT)

            def mm(k, m, sl, jj, par, j, br, start, stop):
                return nc.tensor.matmul(ps[:, k, br * V2:(br + 1) * V2],
                                        m[:, sl, jj, k * P:(k + 1) * P].bitcast(F8),
                                        rhs[:, par, j, br, :], start=start, stop=stop,
                                        skip_group_check=True)

            def chunk_made(hp, par, c):
                wait_alone(pe, "pe", s.rhs_step, RS * (NB * (2 * hp + par) + c + 1))

            pe.wait_ge(s.first_made, 2)
            with pe.Fori(0, H // 2) as hp:
                for par in range(2):
                    with pe.Fori(0, NB) as b:
                        g = (2 * hp + par) * NB + b
                        chunk_made(hp, par, 0)
                        wait_alone(pe, "pe", s.neg_made, NQ * g + 1)
                        for k in range(BLK):
                            wait_alone(pe, "pe", s.bank_free, BLK * g + k + 1)
                            for jj in range(2):
                                p_ = mm(k, pos, SLOT[0], jj, par, jj, 0, jj == 0, False)
                            if k == BLK - 1:
                                p_.then_inc(s.pos_used, 1)
                            for jj in range(2):
                                n_ = mm(k, neg, SLOT[0], jj, par, jj, 1, False, False)
                        n_.then_inc(s.neg_used, 1)
                        for q in range(1, NQ - 1):
                            sl = SLOT[q]
                            if q % (NQ // NB) == 0:
                                chunk_made(hp, par, q * NB // NQ)
                            wait_alone(pe, "pe", s.pos_made, NQ * g + q + 1)
                            for jj in range(2):
                                for k in range(BLK):
                                    last = mm(k, pos, sl, jj, par, 2 * q + jj, 0, False, False)
                            last.then_inc(s.pos_used, 1)
                            wait_alone(pe, "pe", s.neg_made, NQ * g + q + 1)
                            for jj in range(2):
                                for k in range(BLK):
                                    last = mm(k, neg, sl, jj, par, 2 * q + jj, 1, False, False)
                            last.then_inc(s.neg_used, 1)
                        q, sl = NQ - 1, SLOT[NQ - 1]
                        wait_alone(pe, "pe", s.neg_made, NQ * g + q + 1)
                        for k in range(BLK):
                            for jj in range(2):
                                mm(k, pos, sl, jj, par, 2 * q + jj, 0, False, False)
                            for jj in range(2):
                                last = mm(k, neg, sl, jj, par, 2 * q + jj, 1, False, jj == 1)
                            last.then_inc(s.bank_ready, 1)
            def output_tile(t, r, u):
                pe.wait_ge(hT_loaded[u], 2 * (r + 1) * DMA)
                if not isinstance(t, int):
                    pe.wait_ge(s.z_made, 2 * (t - 1))
                for n in range(2):
                    project(2 * u + n, hT_hi[:, u, :], hT_lo[:, u, :], o_hi, o_lo, n)\
                        .then_inc(s.o_written, 1)

            pe.wait_ge(s.bank_free, BLK * (G + 1))
            pe.wait_ge(s.wo_loaded, DMA)
            for u in range(2):
                output_tile(u, 0, u)
            with pe.Fori(1, NT // 2) as r:
                for u in range(2):
                    output_tile(2 * r + u, r, u)


_INS = ["x", "adj", "L0_gnn_W_seq", "L0_gnn_a1", "L0_gnn_a2", "L0_gnn_W_out", "L0_gnn_b_out"]


def kernel(**inputs):
    import numpy as _np
    import concourse.bacc as _bacc
    from concourse.bass_utils import run_bass_kernel_spmd as _run

    nc = _bacc.Bacc("TRN2", target_bir_lowering=False, num_devices=1)
    arrays, args = {}, []
    for name in _INS:
        a = _np.ascontiguousarray(inputs[name])
        arrays[f"in_{name}"] = a
        args.append(nc.dram_tensor(f"in_{name}", a.shape, mybir.dt.from_np(a.dtype), kind="ExternalInput").ap())
    out = nc.dram_tensor("out", (N, D), F32, kind="ExternalOutput").ap()
    build(nc, *args, out)
    r = _run(nc, [arrays], core_ids=[0])
    return r.results[0]["out"]
```
